# Optimizing a Trainium2 kernel written in Bass

```python
import numpy as np
import jax
import jax.numpy as jnp

def _softmax(x, axis=-1):
    return jax.nn.softmax(x, axis=axis)

def _gelu(x):
    return jax.nn.gelu(x, approximate=True)

def _silu(x):
    return jax.nn.silu(x)

def _sigmoid(x):
    return jax.nn.sigmoid(x)

def _layernorm(x, axis=-1, eps=1e-05):
    m = jnp.mean(x, axis=axis, keepdims=True)
    v = jnp.var(x, axis=axis, keepdims=True)
    return (x - m) / jnp.sqrt(v + eps)

def _scatter_add(tgt, idx, src, axis=0):
    return tgt.at[idx].add(src)

def _segment_sum(src, seg, n):
    return jax.ops.segment_sum(src, seg, n)
kernel_name = 'mk_prb_d1_jaxref_r4_1b7da6'

def setup_inputs(seed: int=0):
    np.random.seed(seed)
    _w = jnp.asarray

    def _L0_attn_setup():
        import jax, jax.numpy as jnp
        import numpy as np
        from jax import lax
        H = 64
        P = 64
        N = 128
        G = 8
        K = 4
        D_MODEL = 1024
        I = H * P
        GN = G * N
        CONV_DIM = I + 2 * GN
        PROJ = I + CONV_DIM + H
        EPS = 1e-05
        GROUP_SIZE = I // G

        def _reference_tuple_inner(hidden_states, in_proj_w, conv_weight, conv_bias, dt_bias, A_log, D, norm_weight, out_proj_w):
            B, L, _ = hidden_states.shape
            proj = jnp.einsum('bld,pd->blp', hidden_states, in_proj_w)
            gate = proj[..., :I]
            hbc = proj[..., I:I + CONV_DIM]
            dt = proj[..., -H:]
            pad = jnp.pad(hbc, ((0, 0), (K - 1, 0), (0, 0)))
            conv = conv_bias
            for k in range(K):
                conv = conv + pad[:, k:k + L, :] * conv_weight[:, k]
            xBC = jax.nn.silu(conv)
            x = xBC[..., :I].reshape(B, L, H, P)
            Bm = xBC[..., I:I + GN].reshape(B, L, G, N)
            Cm = xBC[..., I + GN:].reshape(B, L, G, N)
            hpg = H // G
            B_h = jnp.repeat(Bm, hpg, axis=2)
            C_h = jnp.repeat(Cm, hpg, axis=2)
            dt_p = jax.nn.softplus(dt + dt_bias)
            A = -jnp.exp(A_log)
            dA = jnp.exp(dt_p * A)
            dtx = dt_p[..., None] * x

            def step(state, inp):
                dA_t, dtx_t, B_t, C_t = inp
                state = state * dA_t[..., None, None] + dtx_t[..., None] * B_t[:, :, None, :]
                y_t = jnp.einsum('bhpn,bhn->bhp', state, C_t)
                return (state, y_t)
            xs = (jnp.moveaxis(dA, 1, 0), jnp.moveaxis(dtx, 1, 0), jnp.moveaxis(B_h, 1, 0), jnp.moveaxis(C_h, 1, 0))
            state0 = jnp.zeros((B, H, P, N), jnp.float32)
            final_state, ys = lax.scan(step, state0, xs)
            y = jnp.moveaxis(ys, 0, 1) + x * D[None, None, :, None]
            y = y.reshape(B, L, I)
            yg = y.reshape(B, L, G, GROUP_SIZE)
            var = jnp.mean(yg * yg, axis=-1, keepdims=True)
            yn = (yg * lax.rsqrt(var + EPS)).reshape(B, L, I) * norm_weight
            yn = yn * jax.nn.silu(gate)
            out = jnp.einsum('bli,di->bld', yn, out_proj_w)
            conv_state_new = jnp.moveaxis(hbc[:, L - (K - 1):, :], 1, 2)
            return (out, conv_state_new, final_state)
        key = jax.random.key(seed)
        ks = jax.random.split(key, 6)
        B, L = (2, 512)
        s = 0.02
        return {'hidden_states': jax.random.normal(ks[0], (B, L, D_MODEL), jnp.float32), 'in_proj_w': jax.random.normal(ks[1], (PROJ, D_MODEL), jnp.float32) * s, 'conv_weight': jax.random.normal(ks[2], (CONV_DIM, K), jnp.float32) * s, 'conv_bias': jnp.zeros((CONV_DIM,), jnp.float32), 'dt_bias': jnp.ones((H,), jnp.float32), 'A_log': jnp.log(jnp.arange(1, H + 1, dtype=jnp.float32)), 'D': jnp.ones((H,), jnp.float32), 'norm_weight': jnp.ones((I,), jnp.float32), 'out_proj_w': jax.random.normal(ks[3], (D_MODEL, I), jnp.float32) * s}
    _L0_attn_in = _L0_attn_setup()

    def _L0_ffn_setup():
        import jax, jax.numpy as jnp
        import numpy as np
        NUM_EXPERTS = 8
        TOP_K = 2
        RANK = 16
        LORA_ALPHA = 32
        SCALING = LORA_ALPHA / RANK
        key = jax.random.key(seed)
        ks = jax.random.split(key, 6)
        B, S, D_IN, D_OUT = (4, 512, 1024, 1024)
        x = jax.random.normal(ks[0], (B, S, D_IN), dtype=jnp.float32)
        W_base = jax.random.normal(ks[1], (D_OUT, D_IN), dtype=jnp.float32) * 0.02
        b_base = jax.random.normal(ks[2], (D_OUT,), dtype=jnp.float32) * 0.02
        W_router = jax.random.normal(ks[3], (NUM_EXPERTS, D_IN), dtype=jnp.float32) * 0.02
        A = jax.random.normal(ks[4], (NUM_EXPERTS, RANK, D_IN), dtype=jnp.float32) * 0.02
        Bm = jax.random.normal(ks[5], (D_OUT, RANK), dtype=jnp.float32) * 0.02
        Bm = jnp.broadcast_to(Bm, (NUM_EXPERTS, D_OUT, RANK)) * jnp.arange(1, NUM_EXPERTS + 1, dtype=jnp.float32)[:, None, None] * 0.2
        return {'x': x, 'W_base': W_base, 'b_base': b_base, 'W_router': W_router, 'A': A, 'B': Bm}
    _L0_ffn_in = _L0_ffn_setup()
    _d = {'L0_attn_hidden_states': _L0_attn_in['hidden_states'], 'L0_attn_in_proj_w': _L0_attn_in['in_proj_w'], 'L0_attn_conv_weight': _L0_attn_in['conv_weight'], 'L0_attn_conv_bias': _L0_attn_in['conv_bias'], 'L0_attn_dt_bias': _L0_attn_in['dt_bias'], 'L0_attn_A_log': _L0_attn_in['A_log'], 'L0_attn_D': _L0_attn_in['D'], 'L0_attn_norm_weight': _L0_attn_in['norm_weight'], 'L0_attn_out_proj_w': _L0_attn_in['out_proj_w'], 'L0_ffn_W_base': _L0_ffn_in['W_base'], 'L0_ffn_b_base': _L0_ffn_in['b_base'], 'L0_ffn_W_router': _L0_ffn_in['W_router'], 'L0_ffn_A': _L0_ffn_in['A'], 'L0_ffn_B': _L0_ffn_in['B']}
    _x0 = _d['L0_attn_hidden_states']
    _d['L0_attn_hidden_states'] = jax.random.normal(jax.random.fold_in(jax.random.key(seed), 1), (1, 2048, 1024), dtype=_x0.dtype)
    del _x0
    return _d

def reference(L0_attn_hidden_states, L0_attn_in_proj_w, L0_attn_conv_weight, L0_attn_conv_bias, L0_attn_dt_bias, L0_attn_A_log, L0_attn_D, L0_attn_norm_weight, L0_attn_out_proj_w, L0_ffn_W_base, L0_ffn_b_base, L0_ffn_W_router, L0_ffn_A, L0_ffn_B):

    def _L0_attn_ref(hidden_states, in_proj_w, conv_weight, conv_bias, dt_bias, A_log, D, norm_weight, out_proj_w):
        import jax, jax.numpy as jnp
        import numpy as np
        from jax import lax
        H = 64
        P = 64
        N = 128
        G = 8
        K = 4
        D_MODEL = 1024
        I = H * P
        GN = G * N
        CONV_DIM = I + 2 * GN
        PROJ = I + CONV_DIM + H
        EPS = 1e-05
        GROUP_SIZE = I // G

        def _reference_tuple_inner(hidden_states, in_proj_w, conv_weight, conv_bias, dt_bias, A_log, D, norm_weight, out_proj_w):
            B, L, _ = hidden_states.shape
            proj = jnp.einsum('bld,pd->blp', hidden_states, in_proj_w)
            gate = proj[..., :I]
            hbc = proj[..., I:I + CONV_DIM]
            dt = proj[..., -H:]
            pad = jnp.pad(hbc, ((0, 0), (K - 1, 0), (0, 0)))
            conv = conv_bias
            for k in range(K):
                conv = conv + pad[:, k:k + L, :] * conv_weight[:, k]
            xBC = jax.nn.silu(conv)
            x = xBC[..., :I].reshape(B, L, H, P)
            Bm = xBC[..., I:I + GN].reshape(B, L, G, N)
            Cm = xBC[..., I + GN:].reshape(B, L, G, N)
            hpg = H // G
            B_h = jnp.repeat(Bm, hpg, axis=2)
            C_h = jnp.repeat(Cm, hpg, axis=2)
            dt_p = jax.nn.softplus(dt + dt_bias)
            A = -jnp.exp(A_log)
            dA = jnp.exp(dt_p * A)
            dtx = dt_p[..., None] * x

            def step(state, inp):
                dA_t, dtx_t, B_t, C_t = inp
                state = state * dA_t[..., None, None] + dtx_t[..., None] * B_t[:, :, None, :]
                y_t = jnp.einsum('bhpn,bhn->bhp', state, C_t)
                return (state, y_t)
            xs = (jnp.moveaxis(dA, 1, 0), jnp.moveaxis(dtx, 1, 0), jnp.moveaxis(B_h, 1, 0), jnp.moveaxis(C_h, 1, 0))
            state0 = jnp.zeros((B, H, P, N), jnp.float32)
            final_state, ys = lax.scan(step, state0, xs)
            y = jnp.moveaxis(ys, 0, 1) + x * D[None, None, :, None]
            y = y.reshape(B, L, I)
            yg = y.reshape(B, L, G, GROUP_SIZE)
            var = jnp.mean(yg * yg, axis=-1, keepdims=True)
            yn = (yg * lax.rsqrt(var + EPS)).reshape(B, L, I) * norm_weight
            yn = yn * jax.nn.silu(gate)
            out = jnp.einsum('bli,di->bld', yn, out_proj_w)
            conv_state_new = jnp.moveaxis(hbc[:, L - (K - 1):, :], 1, 2)
            return (out, conv_state_new, final_state)
        return _reference_tuple_inner(hidden_states, in_proj_w, conv_weight, conv_bias, dt_bias, A_log, D, norm_weight, out_proj_w)[0]

    def _L0_ffn_ref(x, W_base, b_base, W_router, A, B):
        import jax, jax.numpy as jnp
        import numpy as np
        NUM_EXPERTS = 8
        TOP_K = 2
        RANK = 16
        LORA_ALPHA = 32
        SCALING = LORA_ALPHA / RANK
        bs, seq, d_in = x.shape
        T = bs * seq
        xf = x.reshape(T, d_in)
        base = xf @ W_base.T + b_base
        logits = xf @ W_router.T
        rw, sel = jax.lax.top_k(logits, TOP_K)
        rw = jax.nn.softmax(rw, axis=-1)
        onehot = jax.nn.one_hot(sel, NUM_EXPERTS, dtype=rw.dtype)
        w = jnp.einsum('tk,tke->te', rw, onehot)
        h = jnp.einsum('td,erd->ter', xf, A)
        lora = jnp.einsum('ter,te,eor->to', h, w, B) * SCALING
        return (base + lora).reshape(bs, seq, -1)
    x = L0_attn_hidden_states
    xn = _layernorm(x, axis=-1)
    x = x + _L0_attn_ref(xn, L0_attn_in_proj_w, L0_attn_conv_weight, L0_attn_conv_bias, L0_attn_dt_bias, L0_attn_A_log, L0_attn_D, L0_attn_norm_weight, L0_attn_out_proj_w) + _L0_ffn_ref(xn, L0_ffn_W_base, L0_ffn_b_base, L0_ffn_W_router, L0_ffn_A, L0_ffn_B)
    return x

_drawn_inputs = setup_inputs


def setup_inputs(seed=0):
    import zlib

    import numpy as np

    out = dict(_drawn_inputs(seed))
    spreads = {'L0_attn_conv_bias': (0.0, 0.1),
     'L0_attn_dt_bias': (1.0, 0.6),
     'L0_attn_D': (1.0, 0.2),
     'L0_attn_norm_weight': (1.0, 0.2)}
    factors = {'L0_attn_A_log': 8.0, 'L0_ffn_b_base': 3.958}
    for name, (base, spread) in spreads.items():
        noise = np.random.default_rng([zlib.crc32(name.encode()), seed]).standard_normal(out[name].shape)
        drawn = base * np.exp(spread * noise) if base else spread * noise
        out[name] = jnp.asarray(drawn.astype(out[name].dtype))
    for name, factor in factors.items():
        out[name] = (out[name] * factor).astype(out[name].dtype)
    return out
```

```python
import concourse.bass as bass
from concourse import mybir
from contextlib import ExitStack

F32 = mybir.dt.float32
F32R = mybir.dt.float32r
BF16 = mybir.dt.bfloat16
U32 = mybir.dt.uint32
ALU = mybir.AluOpType
ACT = mybir.ActivationFunctionType

L, DM, H, P, N, G = 2048, 1024, 64, 64, 128, 8
I = H * P
HPG = H // G
GC = I // G
TB = 512
NQ = L // TB
Q = 128
NC = TB // Q
KD = DM // 128
XT = GC // 128
NSET = XT + 2
KZ = GC // 128
OT = DM // 128
NE, RANK = 8, 16
EPS = 1e-5
LOG_ZERO = -104.0
NCONST = NSET * 4 + NSET + XT

PER_G = 14
SLOTS = 1 + NSET + 10 + 6 * PER_G + 17 + 4
K_DT, K_FIRST = 0, 1
K_X = 11
K_OUT = 7
K_TAIL = 20


def k_gate(g_is_0, j):
    return (7 if g_is_0 else 3) + j


NO_GROUP = -1

CR_DENSE, CR_EVAC, CR_2 = 4, 2, 2


def layer_kernel(nc, x_tok, x_tr, w_slots, group_const, dt_bias, a_log, d_skip, b_base, lora_b, out_tr):
    ctx = ExitStack()
    with ctx:
        def sb(name, shape, dt=F32):
            return ctx.enter_context(nc.sbuf_tensor(name, shape, dt))

        def pb(name):
            return ctx.enter_context(nc.psum_tensor(name, [128, 512], F32))

        def sem(name):
            return ctx.enter_context(nc.semaphore(name))

        xn_hi = sb("xn_hi", [128, KD, TB], F32R)
        xn_lo = sb("xn_lo", [128, KD, TB], F32R)
        w_raw = [sb(f"w_raw{i}", [128, 1024]) for i in range(2)]
        w_hi = [sb(f"w_hi{i}", [128, 1024], F32R) for i in range(2)]
        w_lo = [sb(f"w_lo{i}", [128, 1024], F32R) for i in range(2)]
        xT = [sb(f"xT{i}", [128, XT, TB]) for i in range(2)]
        BT = [sb(f"BT{i}", [128, TB]) for i in range(2)]
        CT = [sb(f"CT{i}", [128, TB]) for i in range(2)]
        gate = sb("gate", [128, XT, TB])
        conv_in = [sb(f"conv_in{i}", [128, TB + 3]) for i in range(2)]
        conv_u = [sb(f"conv_u{i}", [128, TB]) for i in range(2)]
        S_all = sb("S_all", [128, G, GC])
        S_cur = sb("S_cur", [128, GC])
        S_dec = sb("S_dec", [128, GC])
        acc = sb("acc", [128, OT, TB])
        z_hi = sb("z_hi", [128, XT, TB], F32R)
        z_lo = sb("z_lo", [128, XT, TB], F32R)
        z_t = sb("z_t", [128, XT, Q])
        x_ck = sb("x_ck", [128, GC])
        B_ck = sb("B_ck", [128, N])
        CBm = sb("CBm", [128, Q])
        E = sb("E", [128, HPG, Q])
        dtx = sb("dtx", [128, GC])
        wx = sb("wx", [128, GC])
        xD = sb("xD", [128, GC])
        y = sb("y", [128, GC])
        sq_junk = sb("sq_junk", [128, GC], BF16)
        yn = [sb(f"yn{i}", [128, GC]) for i in range(2)]
        ssq = sb("ssq", [128, 1])
        rstd = sb("rstd", [128, 2])
        d_rhs = [sb(f"d_rhs{i}", [2 + 2 * HPG, HPG * Q], F32R) for i in range(2)]
        d_lhs = sb("d_lhs", [2 + 2 * HPG, TB], F32R)
        w_tok = sb("w_tok", [128, TB])
        lora_sb = sb("lora_sb", [128, DM])
        tok = sb("tok", [128, 4 * NC, H])
        tok_g = sb("tok_g", [128, 4 * NC, HPG])
        D_all = sb("D_all", [128, H])
        D_g = sb("D_g", [128, HPG])
        consts = sb("consts", [128, G + 1, NCONST])
        const_g = sb("const_g", [128, NCONST])
        halo = sb("halo", [128, G + 1, NSET, 3])
        halo_in = sb("halo_in", [128, NSET, 3])
        halo_out = sb("halo_out", [128, NSET, 3])
        x_in = [sb(f"x_in{i}", [128, DM]) for i in range(2)]
        cum_hi = sb("cum_hi", [H, TB], F32R)
        cum_lo = sb("cum_lo", [H, TB], F32R)
        ident = sb("ident", [128, 128])
        causal = sb("causal", [128, 128])
        ones = sb("ones", [128, 128])
        iota = sb("iota", [128, NE])
        eps_t = sb("eps_t", [128, 2])
        dtb = sb("dtb", [H, 1])
        A_neg = sb("A_neg", [H, 1])
        bb = sb("bb", [128, OT])
        stats = sb("stats", [128, NC, 2, 6])
        ln_sync = sb("ln_sync", [128, NC])
        mv = sb("mv", [128, NC, 2])
        ln_r = sb("ln_r", [128, NC, 2])
        m8 = sb("m8", [128, NC, 8])
        ix8 = sb("ix8", [128, NC, 8], U32)
        ixf = sb("ixf", [128, NC, 2])
        pr = sb("pr", [128, 4, NC])
        rw = sb("rw", [128, 3, NC, NE])
        t_v, t_e, t_p, t_r, t_z, t_z2 = (t[0:H, :] for t in (dtx, wx, xD, y, yn[0], yn[1]))
        E_flat = E[:].rearrange("p h t -> p (h t)")
        t_dt, t_a = E_flat[0:H, 0:TB], E_flat[0:H, TB:2 * TB]
        t_cum = x_ck[0:H, :]
        t_ecum = z_t[0:H].rearrange("p j t -> p (j t)")
        t_diag = y[0:H, 0:NC * H].rearrange("p (c h) -> p c h", c=NC)
        xn = [gate[:, 2 * i:2 * i + 2, :].rearrange("p a b -> p (a b)") for i in range(2)]
        cum_dram = nc.dram_tensor("cum_scratch", [2, H, TB], F32).ap()

        bank = [pb("dense0"), pb("dense1")]
        pX, pCB, pD0, pD1, pY, pS = pb("pX"), pb("pCB"), pb("pD0"), pb("pD1"), pb("pY"), pb("pS")
        pD = [pD0, pD1]
        ln_banks = [pX, pCB, pD0, pD1]

        const_loaded = sem("const_loaded")
        const_made = sem("const_made")
        const_vec = sem("const_vec")
        const_act = sem("const_act")
        w_loaded = [sem("w_loaded0"), sem("w_loaded1")]
        hi_done = sem("hi_done")
        lo0_done = sem("lo0_done")
        lo1_done = sem("lo1_done")
        dense_done = sem("dense_done")
        evac_act = sem("evac_act")
        evac_dve = sem("evac_dve")
        x_loaded = [sem("x_loaded0"), sem("x_loaded1")]
        ln_stat = sem("ln_stat")
        ln_rstd = sem("ln_rstd")
        xn_done = sem("xn_done")
        lnT_done = sem("lnT_done")
        xn_hi_done = sem("xn_hi_done")
        xn_lo_done = sem("xn_lo_done")
        dt_act = sem("dt_act")
        dt_dve = sem("dt_dve")
        rt_dve = sem("rt_dve")
        tokT_done = sem("tokT_done")
        tok_ready = sem("tok_ready")
        wT_done = sem("wT_done")
        w_tok_ready = sem("w_tok_ready")
        cum_stored = sem("cum_stored")
        rhs_loaded = [sem("rhs_loaded0"), sem("rhs_loaded1")]
        lhs_loaded = sem("lhs_loaded")
        acc_loaded = sem("acc_loaded")
        out_stored = sem("out_stored")
        prep_done = sem("prep_done")
        taps = sem("taps")
        tanh_done = sem("tanh_done")
        post = sem("post")
        gate_done = sem("gate_done")
        s1 = sem("s1")
        ck_evac = sem("ck_evac")
        relu_done = sem("relu_done")
        exp_done = sem("exp_done")
        cbm_done = sem("cbm_done")
        m_done = sem("m_done")
        xw_done = sem("xw_done")
        xd_done = sem("xd_done")
        sdec_done = sem("sdec_done")
        s_upd = sem("s_upd")
        s2 = sem("s2")
        st_done = sem("st_done")
        y_step = sem("y_step")
        sq_done = sem("sq_done")
        rstd_done = sem("rstd_done")
        yn_done = sem("yn_done")
        s3 = sem("s3")
        z_done = sem("z_done")
        zhi_done = sem("zhi_done")

        def slot(q, g, k):
            return q * SLOTS + g * PER_G + k

        def dense_n(q, g, k, h):
            return q * (2 * SLOTS) + g * (2 * PER_G) + (2 * k + h + 1 + CR_DENSE)

        def act_n(q, g, j):
            return q * 81 + g * 10 + (7 + j + 1 + CR_EVAC)

        def out_n(q, g, i):
            return q * 73 + g * 8 + (i - 8 + 1 + CR_EVAC)

        def ffn_n(q, j):
            return q * 73 + (56 + j + 1 + CR_EVAC)

        def tail_n(q, i):
            return q * 73 + (65 + i + 1 + CR_EVAC)

        def grp(q, g):
            return q * G + g

        def chunk(q, g, c):
            return q * (G * NC) + g * NC + c

        def post_n(q, g, j):
            return q * (G * NSET) + g * NSET + (j + 1)

        DT_ACT, DT_DVE, RT_DVE = 9, 21, 19

        block = ctx.enter_context(nc.Block())

        @block.sync
        def _(sp):
            for t, src in ((consts, group_const), (D_all, d_skip), (bb, b_base), (lora_sb, lora_b),
                           (dtb, dt_bias), (A_neg, a_log)):
                sp.dma_start(t[:], src).then_inc(const_loaded, 16)
            for s in range(2):
                sp.dma_start(w_raw[s][:], w_slots[s]).then_inc(w_loaded[s], 16)
            with sp.Fori(0, NQ) as q:
                def load_x(i):
                    sp.wait_ge(xn_done, q * NC + (i - 1 + CR_2))
                    sp.dma_start(x_in[i % 2][:], x_tok[bass.ds(q * TB + i * 128, 128), :]).then_inc(x_loaded[i % 2], 16)

                def load_w(n, s):
                    sp.wait_ge(lo0_done, q * SLOTS + n - 1)
                    sp.wait_ge(lo1_done, q * SLOTS + n - 1)
                    sp.dma_start(w_raw[s][:], w_slots[n]).then_inc(w_loaded[s], 16)

                load_x(0)
                load_x(1)
                load_w(2, 0)
                load_w(3, 1)
                load_x(2)
                load_x(3)
                with sp.Fori(2, SLOTS // 2 + 1) as pair:
                    for s in range(2):
                        sp.wait_ge(lo0_done, q * SLOTS + pair * 2 + (s - 1))
                        sp.wait_ge(lo1_done, q * SLOTS + pair * 2 + (s - 1))
                        sp.dma_start(w_raw[s][:], w_slots[bass.ds(pair * 2 + s, 1)].rearrange("o p f -> (o p) f"))\
                          .then_inc(w_loaded[s], 16)
            sp.wait_ge(out_stored, 16 + NQ * 64)

        @block.gpsimd
        def _(pool):
            pool.sem_inc(xd_done, 1)
            n_made = 0

            def made(ins):
                nonlocal n_made
                n_made += 1
                ins.then_inc(const_made, 1)

            ind = E[0:2 + 2 * HPG]
            made(nc.gpsimd.memset(ident[:], 0.0))
            made(nc.gpsimd.memset(causal[:], 1.0))
            made(nc.gpsimd.memset(ones[:], 1.0))
            made(nc.gpsimd.memset(ind, 0.0))
            made(nc.gpsimd.memset(S_all[:], 0.0))
            made(nc.gpsimd.memset(halo[:], 0.0))
            made(nc.gpsimd.memset(halo_out[:], 0.0))
            made(nc.gpsimd.memset(eps_t[:, 0:1], EPS))
            made(nc.gpsimd.memset(eps_t[:, 1:2], -0.5))
            for e in range(NE):
                made(nc.gpsimd.memset(iota[:, e:e + 1], float(e)))
            pool.wait_ge(const_made, n_made)
            made(nc.gpsimd.affine_select(out=ident[:], in_=ident[:], compare_op=ALU.not_equal, fill=1.0, base=0,
                                         pattern=[[-1, 128]], channel_multiplier=1))
            made(nc.gpsimd.affine_select(out=causal[:], in_=causal[:], compare_op=ALU.is_ge, fill=0.0, base=0,
                                         pattern=[[1, 128]], channel_multiplier=-1))
            for first in (2, 2 + HPG):
                pool.wait_ge(const_made, n_made)
                made(nc.gpsimd.affine_select(out=ind, in_=ind, compare_op=ALU.not_equal, fill=-1.0, base=-first,
                                             pattern=[[-1, HPG], [0, Q]], channel_multiplier=1))
            assert n_made == 21

            def lo_first_half(s, n):
                pool.wait_ge(hi_done, n)
                nc.gpsimd.tensor_tensor(w_lo[s][:, 0:512], w_raw[s][:, 0:512], w_hi[s][:, 0:512].bitcast(F32),
                                        ALU.subtract).then_inc(lo0_done, 1)

            for s in range(2):
                lo_first_half(s, 2 * s + 1)

            def block_body(q):
                def lo(g, k):
                    lo_first_half(k % 2, q * (2 * SLOTS) + g * (2 * PER_G) + (2 * (k + 2) + 1))

                def chunk_pre(g, c):
                    n = chunk(q, g, c)
                    if c == 0:
                        pool.wait_ge(prep_done, q * 9 + g + 2)
                    pool.wait_ge(y_step, n * 3 + CR_2)
                    pool.wait_ge(ck_evac, n * 2 + 1)
                    nc.gpsimd.tensor_tensor(xD[:].rearrange("t (h p) -> t h p", h=HPG),
                                            x_ck[:].rearrange("t (h p) -> t h p", h=HPG),
                                            D_g[:].unsqueeze(2).broadcast_to([128, HPG, P]), ALU.mult)\
                        .then_inc(xd_done, 1)
                    pool.wait_ge(s_upd, grp(q, g) * 6 + (c + 1 + 1))
                    nc.gpsimd.tensor_tensor(S_dec[:].rearrange("n (h p) -> n h p", h=HPG),
                                            S_cur[:].rearrange("n (h p) -> n h p", h=HPG),
                                            tok_g[:, 3 * NC + c, :].unsqueeze(2).broadcast_to([128, HPG, P]), ALU.mult)\
                        .then_inc(sdec_done, 1)

                def inv_rms(g, c):
                    n = chunk(q, g, c)
                    pool.wait_ge(sq_done, n + 1 + 1)
                    nc.gpsimd.tensor_tensor(rstd[:, 0:1], ssq[:], eps_t[:, 0:1], ALU.add).then_inc(rstd_done, 1)
                    pool.wait_ge(rstd_done, n * 2 + 1)
                    nc.gpsimd.tensor_tensor(rstd[:, 1:2], rstd[:, 0:1], eps_t[:, 1:2], ALU.pow).then_inc(rstd_done, 1)

                for i in range(NC):
                    n = q * NC + i
                    pool.wait_ge(ln_stat, n * 4 + 4)
                    nc.gpsimd.tensor_tensor(ln_r[:, i, 0:1], mv[:, i, 1:2], eps_t[:, 0:1], ALU.add).then_inc(ln_rstd, 1)
                    pool.wait_ge(ln_rstd, n * 2 + 1)
                    nc.gpsimd.tensor_tensor(ln_r[:, i, 1:2], ln_r[:, i, 0:1], eps_t[:, 1:2], ALU.pow).then_inc(ln_rstd, 1)
                lo(0, K_DT)
                for j in range(NSET):
                    lo(0, K_FIRST + j)

                def group(g, first=False, last=False):
                    lo(g, k_gate(first, 0))
                    lo(g, k_gate(first, 1))
                    chunk_pre(g, 0)
                    lo(g, k_gate(first, 2))
                    lo(g, k_gate(first, 3))
                    if not first:
                        lo(g, K_OUT)
                    inv_rms(g, 0)
                    chunk_pre(g, 1)
                    if not first:
                        lo(g, K_OUT + 1)
                        lo(g, K_OUT + 2)
                        lo(g, K_OUT + 3)
                    inv_rms(g, 1)
                    chunk_pre(g, 2)
                    n_x = [3, 1, 2] if last else [2, 1, 2]
                    k = K_X
                    for _ in range(n_x[0] + n_x[1]):
                        lo(g, k)
                        k += 1
                    inv_rms(g, 2)
                    chunk_pre(g, 3)
                    while k < K_X + (9 if last else 6):
                        lo(g, k)
                        k += 1
                    inv_rms(g, 3)

                group(0, first=True)
                with pool.Fori(0, 3) as pair:
                    group(pair * 2 + 1)
                    group(pair * 2 + 2)
                group(7, last=True)
                for m in range(4):
                    lo(7, K_TAIL + m)

            with pool.Fori(0, NQ) as q:
                block_body(q)

        @block.scalar
        def _(act):
            act.sem_inc(evac_act, CR_EVAC)
            act.sem_inc(sq_done, 1)
            act.sem_inc(out_stored, 16)
            act.wait_ge(const_loaded, 96)
            nc.scalar.activation(A_neg[:], A_neg[:], ACT.Exp).then_inc(const_act, 1)

            def split_hi(s, h):
                sl = slice(512 * h, 512 * h + 512)
                nc.scalar.activation(w_hi[s][:, sl], w_raw[s][:, sl], ACT.Copy).then_inc(hi_done, 1)

            for s in range(2):
                act.wait_ge(w_loaded[s], 16)
                split_hi(s, 0)
                split_hi(s, 1)

            def block_body(q):
                n_dt = 0

                def dt_step(ins):
                    nonlocal n_dt
                    n_dt += 1
                    ins.then_inc(dt_act, 1)

                def dt_wait():
                    act.wait_ge(dt_act, q * DT_ACT + n_dt)

                def split(g, k):
                    s = k % 2
                    act.wait_ge(w_loaded[s], (q * (SLOTS // 2) + g * (PER_G // 2) + ((k + 2) // 2 + 1)) * 16)
                    for h in range(2):
                        act.wait_ge(dense_done, dense_n(q, g, k, h))
                        split_hi(s, h)

                def ev_conv(g, k, j, b):
                    r = j % 2
                    act.wait_ge(dense_done, dense_n(q, g if k >= K_X else 0, k, 1))
                    if j >= 2:
                        act.wait_ge(post, post_n(q, g + 1, j - 2))
                    elif k >= K_X:
                        act.wait_ge(gate_done, grp(q, g) * XT + (j + 2 + 1))
                    if j == 0:
                        act.wait_ge(prep_done, q * 9 + g + 2)
                    nc.scalar.activation(conv_in[r][:, 3:3 + TB], bank[b][:], ACT.Copy)
                    nc.scalar.activation(conv_u[r][:], bank[b][:], ACT.Identity, bias=const_g[:, 24 + j:25 + j],
                                         scale=const_g[:, 4 * j + 3:4 * j + 4]).then_inc(evac_act, 1)

                def tanh_conv(g, j):
                    act.wait_ge(taps, (post_n(q, g + 1, j)) * 4)
                    nc.scalar.activation(conv_in[j % 2][:, 0:TB], conv_u[j % 2][:], ACT.Tanh).then_inc(tanh_done, 1)

                def ev_gate(g, first, j):
                    k = k_gate(first, j)
                    b = (k if first else k - 4) % 2
                    act.wait_ge(dense_done, dense_n(q, g, k, 1))
                    if j < 2:
                        act.wait_ge(post, post_n(q, g, 4 + j))
                    else:
                        act.wait_ge(gate_done, grp(q, g) * XT + (j - 2 + 1))
                    if j == 0:
                        act.wait_ge(prep_done, q * 9 + g + 2)
                    nc.scalar.activation(conv_in[j % 2][:, 0:TB], bank[b][:], ACT.Tanh, scale=0.5)
                    nc.scalar.activation(conv_u[j % 2][:], bank[b][:], ACT.Copy,
                                         scale=const_g[:, 30 + j:31 + j]).then_inc(evac_act, 1)

                def load_rhs(g, c):
                    act.dma_start(d_rhs[c % 2][0:2, :].bitcast(F32).rearrange("l (h t) -> l h t", h=HPG),
                                  cum_dram[:, bass.ds(g * HPG, HPG), c * Q:(c + 1) * Q]).then_inc(rhs_loaded[c % 2], 16)

                def load_lhs(g):
                    for l in range(2):
                        act.dma_start(d_lhs[2 + HPG * l:2 + HPG * (l + 1), :].bitcast(F32),
                                      cum_dram[l, bass.ds(g * HPG, HPG), :]).then_inc(lhs_loaded, 16)

                def chunk_1(g, c, last=False):
                    n = chunk(q, g, c)
                    act.wait_ge(xd_done, n + 1)
                    act.wait_ge(s1, n * 4 + 1)
                    nc.scalar.activation(x_ck[:], pX[:], ACT.Copy).then_inc(ck_evac, 1)
                    act.wait_ge(s1, n * 4 + 2)
                    nc.scalar.activation(B_ck[:], pCB[:, 0:N], ACT.Copy).then_inc(ck_evac, 1)
                    for h in range(2):
                        act.wait_ge(s1, n * 4 + (3 + h))
                        nc.scalar.activation(E_flat[:, 512 * h:512 * h + 512], pD[h][:], ACT.Relu, scale=-1.0)\
                            .then_inc(relu_done, 1)
                    if c < 2:
                        load_rhs(g, c + 2)
                    elif not last:
                        load_rhs(g + 1, c - 2)
                    if c == 3 and not last:
                        load_lhs(g + 1)
                    for h in range(2):
                        act.wait_ge(relu_done, n * 2 + (h + 1))
                        nc.scalar.activation(E_flat[:, 512 * h:512 * h + 512], E_flat[:, 512 * h:512 * h + 512], ACT.Exp,
                                             scale=-1.0).then_inc(exp_done, 1)

                def mean_square(g, c):
                    n = chunk(q, g, c)
                    act.wait_ge(sq_done, n + 1)
                    act.wait_ge(y_step, n * 3 + (3 + CR_2))
                    nc.scalar.activation(sq_junk[:], y[:], ACT.Square, scale=float(GC) ** -0.5,
                                         accum_out=ssq[:]).then_inc(sq_done, 1)

                def z_high(g, c):
                    act.wait_ge(z_done, chunk(q, g, c) * 2 + (1 + 4))
                    nc.scalar.activation(z_hi[:, :, c * Q:(c + 1) * Q], z_t[:], ACT.Copy).then_inc(zhi_done, 1)

                for i in range(NC):
                    for h in range(2):
                        n = q * (2 * NC) + (2 * i + h + 1)
                        act.wait_ge(lnT_done, n)
                        nc.scalar.activation(xn_hi[:, 4 * h:4 * h + 4, i * 128:(i + 1) * 128],
                                             ln_banks[(2 * i + h) % 4][:].rearrange("p (k t) -> p k t", k=4), ACT.Copy)\
                            .then_inc(xn_hi_done, 1)
                act.wait_ge(out_stored, q * 64 + 16)
                act.dma_start(acc[:], x_tr[:, bass.ds(q * TB, TB)].rearrange("(o p) t -> p o t", p=128))\
                    .then_inc(acc_loaded, 16)
                split(0, K_DT)
                act.wait_ge(dense_done, dense_n(q, 0, K_DT, 1))
                dt_step(nc.scalar.activation(t_v, bank[0][0:H, :], ACT.Identity, bias=dtb[:]))
                nc.scalar.activation(t_e, bank[0][0:H, :], ACT.Abs, bias=dtb[:]).then_inc(evac_act, 1)
                act.wait_ge(evac_act, q * 81 + (1 + CR_EVAC))
                dt_step(nc.scalar.activation(t_e, t_e, ACT.Exp, scale=-1.0))

                def first_unit(j):
                    split(0, K_FIRST + j)
                    if j >= 1:
                        tanh_conv(-1, j - 1)
                    ev_conv(-1, K_FIRST + j, j, (1 + j) % 2)

                first_unit(0)
                first_unit(1)
                act.wait_ge(dt_dve, q * DT_DVE + 18)
                dt_step(nc.scalar.activation(cum_hi[:], t_cum, ACT.Copy))
                dt_step(nc.scalar.activation(t_ecum, t_cum, ACT.Exp))
                for c in range(NC):
                    dt_step(nc.scalar.activation(t_e[:, c * Q:(c + 1) * Q], t_cum[:, c * Q:(c + 1) * Q], ACT.Exp,
                                                 scale=-1.0, bias=t_cum[:, (c + 1) * Q - 1:(c + 1) * Q]))
                dt_wait()
                act.dma_start(cum_dram[0], cum_hi[:].bitcast(F32)).then_inc(cum_stored, 16)
                act.wait_ge(dt_dve, q * DT_DVE + 19)
                act.dma_start(cum_dram[1], cum_lo[:].bitcast(F32)).then_inc(cum_stored, 16)
                first_unit(2)
                act.wait_ge(cum_stored, (q + 1) * 32)
                load_lhs(0)
                load_rhs(0, 0)
                load_rhs(0, 1)
                first_unit(3)
                act.wait_ge(rt_dve, q * RT_DVE + 5)
                dt_step(nc.scalar.activation(pr[:, 1, :], pr[:, 0, :], ACT.Exp))
                first_unit(4)
                for h in range(2):
                    act.wait_ge(tokT_done, q * 2 + (h + 1))
                    nc.scalar.activation(tok[:, 2 * NC * h:2 * NC * (h + 1), :],
                                         pD[h][:].rearrange("p (c h) -> p c h", h=H), ACT.Copy).then_inc(tok_ready, 1)
                first_unit(5)
                act.wait_ge(wT_done, q + 1)
                nc.scalar.activation(w_tok[:], pS[:], ACT.Copy).then_inc(w_tok_ready, 1)
                tanh_conv(-1, 5)
                assert n_dt == DT_ACT, n_dt

                def group(g, first=False, last=False):
                    def gate_unit(j):
                        split(g, k_gate(first, j))
                        ev_gate(g, first, j)

                    def x_unit(j):
                        split(g, K_X + j)
                        if not last:
                            if j >= 1:
                                tanh_conv(g, j - 1)
                            ev_conv(g, K_X + j, j, (K_X + j) % 2)

                    def out_unit(m):
                        if not first:
                            split(g, K_OUT + m)

                    gate_unit(0)
                    gate_unit(1)
                    chunk_1(g, 0, last)
                    split(g, k_gate(first, 2))
                    if not first:
                        z_high(g - 1, 3)
                    ev_gate(g, first, 2)
                    gate_unit(3)
                    out_unit(0)
                    mean_square(g, 0)
                    chunk_1(g, 1, last)
                    out_unit(1)
                    out_unit(2)
                    out_unit(3)
                    mean_square(g, 1)
                    if not first:
                        act.wait_ge(dense_done, dense_n(q, g, K_OUT + 3, 1))
                    z_high(g, 0)
                    chunk_1(g, 2, last)
                    x = [3, 4, 6] if last else [2, 3, 5]
                    for j in range(x[0]):
                        x_unit(j)
                    z_high(g, 1)
                    x_unit(x[0])
                    mean_square(g, 2)
                    chunk_1(g, 3, last)
                    for j in range(x[1], x[2]):
                        x_unit(j)
                    z_high(g, 2)
                    x_unit(x[2])
                    mean_square(g, 3)
                    if last:
                        x_unit(7)
                        x_unit(8)
                    else:
                        tanh_conv(g, 5)

                group(0, first=True)
                with act.Fori(0, 3) as pair:
                    group(pair * 2 + 1)
                    group(pair * 2 + 2)
                group(7, last=True)
                z_high(7, 3)
                for m in range(4):
                    split(7, K_TAIL + m)
                    act.wait_ge(evac_dve, tail_n(q, 2 * m + 1))
                    act.dma_start(out_tr[m * 256:(m + 1) * 256, bass.ds(q * TB, TB)].rearrange("(o p) t -> p o t", p=128),
                                  acc[:, 2 * m:2 * m + 2, :]).then_inc(out_stored, 16)

            with act.Fori(0, NQ) as q:
                block_body(q)

        @block.tensor
        def _(pe):
            pe.sem_inc(dense_done, CR_DENSE)
            pe.wait_ge(const_made, 21)

            def block_body(q):
                def weights(g, k, h):
                    pe.wait_ge(lo0_done if h == 0 else lo1_done, slot(q, g, k) + 1)

                def w(k, t):
                    return (w_hi[k % 2][:, t * 128:(t + 1) * 128], w_lo[k % 2][:, t * 128:(t + 1) * 128])

                def three(out, lhs, rhs, start, stop):
                    nc.tensor.matmul(out, lhs[0], rhs[0], start=start, stop=False)
                    nc.tensor.matmul(out, lhs[0], rhs[1], start=False, stop=False)
                    return nc.tensor.matmul(out, lhs[1], rhs[0], start=False, stop=stop)

                def in_unit(g, k, b, more=None):
                    for h in range(2):
                        weights(g, k, h)
                        for t in range(4 * h, 4 * h + 4):
                            mm = three(bank[b][:], w(k, t), (xn_hi[:, t, :], xn_lo[:, t, :]), t == 0,
                                       t == KD - 1 and more is None)
                        if h == 1 and more is not None:
                            mm = more()
                        mm.then_inc(dense_done, 1)

                def gate_unit(g, first, j):
                    k = k_gate(first, j)
                    pe.wait_ge(evac_act, act_n(q, g - 1, 8 + j) if j < 2 else act_n(q, g, j - 2))
                    in_unit(g, k, (k if first else k - 4) % 2)

                def x_unit(g, first, j):
                    if j >= 2:
                        pe.wait_ge(evac_act, act_n(q, g, 4 + j - 2))
                    elif first:
                        pe.wait_ge(evac_act, act_n(q, g, 2 + j))
                    else:
                        pe.wait_ge(evac_dve, out_n(q, g, 6 + j))
                    in_unit(g, K_X + j, (K_X + j) % 2)

                def ffn_unit(j):
                    pe.wait_ge(evac_dve, out_n(q, 7, 6 + j) if j < 2 else ffn_n(q, j - 2))
                    more = None
                    if j >= 1:
                        def more():
                            pe.wait_ge(evac_dve, ffn_n(q, 0))
                            return nc.tensor.matmul(bank[(K_X + j) % 2][:], lora_sb[:, (j - 1) * 128:j * 128], w_tok[:],
                                                    start=False, stop=True)
                    in_unit(7, K_X + j, (K_X + j) % 2, more)

                def out_units(g, m, tail=False):
                    k = (K_TAIL if tail else K_OUT) + m
                    for h in range(2):
                        i = 2 * m + h
                        if i >= 2:
                            pe.wait_ge(evac_dve, tail_n(q, i - 2) if tail else out_n(q, g, i - 2))
                        elif tail:
                            pe.wait_ge(evac_dve, ffn_n(q, 7 + i))
                        else:
                            pe.wait_ge(evac_act, act_n(q, g, 2 + i))
                        if i == 0:
                            pe.wait_ge(z_done, chunk(q, g if tail else g - 1, 3) * 2 + (2 + 4))
                        weights(g, k, h)
                        b = ((K_TAIL if tail else 3) + i) % 2
                        for t in range(KZ):
                            mm = three(bank[b][:], w(k, 4 * h + t), (z_hi[:, t, :], z_lo[:, t, :]), t == 0, t == KZ - 1)
                        mm.then_inc(dense_done, 1)

                def chunk_1(g, c, p):
                    n = chunk(q, g, c)
                    cs = slice(c * Q, (c + 1) * Q)
                    if c == 0:
                        pe.wait_ge(post, post_n(q, g, NSET - 1))
                    pe.wait_ge(z_done, n * 2 + (4 - 3))
                    for j in range(XT):
                        mm = nc.tensor.transpose(pX[:, j * 128:(j + 1) * 128], xT[p][:, j, cs], ident[:])
                    mm.then_inc(s1, 1)
                    nc.tensor.transpose(pCB[:, 0:N], BT[p][:, cs], ident[:])
                    nc.tensor.matmul(pCB[:, N:N + Q], BT[p][:, cs], CT[p][:, cs], start=True, stop=True).then_inc(s1, 1)
                    if c == 0:
                        pe.wait_ge(lhs_loaded, (grp(q, g) + 1) * 32)
                    pe.wait_ge(rhs_loaded[c % 2], (q * (2 * G) + g * 2 + (c // 2 + 1)) * 16)
                    for h in range(2):
                        nc.tensor.matmul(pD[h][:], d_lhs[:, cs], d_rhs[c % 2][:, 512 * h:512 * h + 512],
                                         start=True, stop=True).then_inc(s1, 1)

                def chunk_2(g, c, p):
                    n = chunk(q, g, c)
                    pe.wait_ge(s_upd, grp(q, g) * 6 + (c + 1 + 1))
                    nc.tensor.matmul(pS[:], CT[p][:, c * Q:(c + 1) * Q], S_cur[:], start=True, stop=True).then_inc(s2, 1)
                    pe.wait_ge(y_step, n * 3 + (0 + CR_2))
                    pe.wait_ge(xw_done, n * 2 + 1)
                    for h in range(HPG):
                        if h % 4 == 0:
                            pe.wait_ge(m_done, n * 2 + (h // 4 + 1))
                        mm = nc.tensor.matmul(pY[:, h * P:(h + 1) * P], E[:, h, :], dtx[:, h * P:(h + 1) * P],
                                              start=True, stop=True)
                    mm.then_inc(s2, 1)

                def chunk_2b(g, c):
                    n = chunk(q, g, c)
                    pe.wait_ge(ck_evac, n * 2 + 2)
                    pe.wait_ge(xw_done, n * 2 + 2)
                    pe.wait_ge(y_step, n * 3 + (1 + CR_2))
                    nc.tensor.matmul(pS[:], B_ck[:], wx[:], start=True, stop=True).then_inc(st_done, 1)

                def chunk_3(g, c, tail=False):
                    n = chunk(q, g, c)
                    if not tail:
                        pe.wait_ge(ck_evac, n * 2 + 3)
                    pe.wait_ge(yn_done, n + 1)
                    for j in range(XT):
                        mm = nc.tensor.transpose(pX[:, j * 128:(j + 1) * 128], yn[c % 2][:, j * 128:(j + 1) * 128], ident[:])
                    mm.then_inc(s3, 1)

                for i in range(NC):
                    pe.wait_ge(xn_done, q * NC + (i + 1 + CR_2))
                    for h in range(2):
                        if i >= 2:
                            pe.wait_ge(xn_lo_done, q * (2 * NC) + (2 * i + h - 4 + 1))
                        for t in range(4):
                            mm = nc.tensor.transpose(ln_banks[(2 * i + h) % 4][:, t * 128:(t + 1) * 128],
                                                     xn[i % 2][:, (4 * h + t) * 128:(4 * h + t + 1) * 128], ident[:])
                        mm.then_inc(lnT_done, 1)
                pe.wait_ge(xn_lo_done, q * (2 * NC) + 2 * NC)
                pe.wait_ge(evac_dve, q * 73 + (-1 + CR_EVAC))
                weights(0, K_DT, 0)
                weights(0, K_DT, 1)
                for t in range(KD):
                    three(bank[0][:], w(K_DT, t), (xn_hi[:, t, :], xn_lo[:, t, :]), t == 0, t == KD - 1)
                for i in range(NC):
                    ts = slice(i * 128, (i + 1) * 128)
                    for t in range(KD):
                        mm = three(pY[:, i * NE:(i + 1) * NE], (xn_hi[:, t, ts], xn_lo[:, t, ts]),
                                   [v[:, H:H + NE] for v in w(K_DT, t)], t == 0, t == KD - 1)
                mm.then_inc(dense_done, 2)
                for j in range(NSET):
                    if j == 0:
                        pe.wait_ge(evac_dve, q * 73 + (0 + CR_EVAC))
                    elif j == 1:
                        pe.wait_ge(evac_act, q * 81 + (1 + CR_EVAC))
                    else:
                        pe.wait_ge(evac_act, act_n(q, -1, 4 + j - 2))
                    in_unit(0, K_FIRST + j, (1 + j) % 2)
                    if j == 3:
                        pe.wait_ge(dt_dve, q * DT_DVE + DT_DVE)
                        nc.tensor.matmul(pD[1][:, NC * H:2 * NC * H], ones[0:H, :], y[0:H, 0:NC * H], start=True, stop=True)
                        for s, src in ((0, t_dt), (1, t_z)):
                            for c in range(NC):
                                mm = nc.tensor.transpose(pD[0][:, (s * NC + c) * H:(s * NC + c + 1) * H],
                                                         src[:, c * Q:(c + 1) * Q], ident[0:H, 0:H])
                        mm.then_inc(tokT_done, 1)
                        for c in range(NC):
                            mm = nc.tensor.transpose(pD[1][:, c * H:(c + 1) * H], t_ecum[:, c * Q:(c + 1) * Q],
                                                     ident[0:H, 0:H])
                        mm.then_inc(tokT_done, 1)
                    if j == 4:
                        pe.wait_ge(rt_dve, q * RT_DVE + RT_DVE)
                        for i in range(NC):
                            mm = nc.tensor.transpose(pS[:, i * 128:(i + 1) * 128], dtx[:, i * 128:(i + 1) * 128], ident[:])
                        mm.then_inc(wT_done, 1)

                def group(g, p, first=False, last=False):
                    def x_units(n):
                        nonlocal j
                        for _ in range(n):
                            ffn_unit(j) if last else x_unit(g, first, j)
                            j += 1

                    def outs(m):
                        if not first:
                            out_units(g, m)

                    j = 0
                    gate_unit(g, first, 0)
                    gate_unit(g, first, 1)
                    chunk_1(g, 0, p)
                    gate_unit(g, first, 2)
                    if not first:
                        chunk_3(g - 1, 3)
                    gate_unit(g, first, 3)
                    chunk_2(g, 0, p)
                    outs(0)
                    chunk_2b(g, 0)
                    chunk_1(g, 1, p)
                    outs(1)
                    outs(2)
                    chunk_2(g, 1, p)
                    chunk_3(g, 0, tail=True)
                    outs(3)
                    chunk_2b(g, 1)
                    chunk_1(g, 2, p)
                    x_units(3 if last else 2)
                    chunk_2(g, 2, p)
                    chunk_3(g, 1)
                    x_units(1)
                    chunk_2b(g, 2)
                    chunk_1(g, 3, p)
                    x_units(2)
                    chunk_2(g, 3, p)
                    chunk_3(g, 2)
                    x_units(1)
                    chunk_2b(g, 3)
                    x_units(2 if last else 0)

                group(0, 0, first=True)
                with pe.Fori(0, 3) as pair:
                    group(pair * 2 + 1, 1)
                    group(pair * 2 + 2, 0)
                group(7, 1, last=True)
                chunk_3(7, 3, tail=True)
                for m in range(4):
                    out_units(7, m, tail=True)

            with pe.Fori(0, NQ) as q:
                block_body(q)

        @block.vector
        def _(dve):
            for s, n in ((evac_dve, CR_EVAC), (xn_done, CR_2), (y_step, CR_2), (z_done, 4), (s_upd, 1)):
                dve.sem_inc(s, n)
            dve.wait_ge(const_loaded, 96)
            nc.vector.tensor_scalar(consts[:], consts[:], 0.5, None, ALU.mult).then_inc(const_vec, 1)
            dve.wait_ge(const_act, 1)
            nc.vector.tensor_scalar(A_neg[:], A_neg[:], -1.0, None, ALU.mult).then_inc(const_vec, 1)
            dve.wait_ge(const_made, 21)
            for b in range(2):
                nc.vector.tensor_copy(d_rhs[b][:], E_flat[0:2 + 2 * HPG, :]).then_inc(const_vec, 1)
            nc.vector.tensor_copy(d_lhs[0:2, 0:TB].rearrange("l (c t) -> l c t", c=NC),
                                  ones[0:2, :].unsqueeze(1).broadcast_to([2, NC, 128])).then_inc(const_vec, 1)
            dve.wait_ge(const_vec, 5)

            def lo_second_half(s, n):
                dve.wait_ge(hi_done, n)
                nc.vector.tensor_tensor(w_lo[s][:, 512:1024], w_raw[s][:, 512:1024], w_hi[s][:, 512:1024].bitcast(F32),
                                        ALU.subtract).then_inc(lo1_done, 1)

            for s in range(2):
                lo_second_half(s, 2 * s + 2)

            def heads(t):
                return t.rearrange("t (h p) -> t h p", h=HPG)

            def per_head(kind, c):
                return tok_g[:, kind * NC + c, :].unsqueeze(2).broadcast_to([128, HPG, P])

            def block_body(q):
                n_dt = n_rt = 0

                def dt_step(ins, wait=True):
                    nonlocal n_dt
                    n_dt += 1
                    ins.then_inc(dt_dve, 1)
                    if wait:
                        dve.wait_ge(dt_dve, q * DT_DVE + n_dt)

                def rt_step(ins, wait=True):
                    nonlocal n_rt
                    n_rt += 1
                    ins.then_inc(rt_dve, 1)
                    if wait:
                        dve.wait_ge(rt_dve, q * RT_DVE + n_rt)

                def lo(g, k):
                    lo_second_half(k % 2, q * (2 * SLOTS) + g * (2 * PER_G) + (2 * (k + 2) + 2))

                def conv_taps(g, j):
                    r, n = j % 2, (post_n(q, g + 1, j) - 1) * 4
                    if j >= 2:
                        dve.wait_ge(post, post_n(q, g + 1, j - 2))
                    elif g is not NO_GROUP:
                        dve.wait_ge(gate_done, grp(q, g) * XT + (j + 2 + 1))
                    nc.vector.tensor_copy(conv_in[r][:, 0:3], halo_in[:, j, :]).then_inc(taps, 1)
                    dve.wait_ge(evac_act, act_n(q, g, 4 + j))
                    nc.vector.tensor_copy(halo_out[:, j, :], conv_in[r][:, TB:TB + 3])
                    for t in range(3):
                        dve.wait_ge(taps, n + t + 1)
                        nc.vector.scalar_tensor_tensor(out=conv_u[r][:], in0=conv_in[r][:, t:t + TB],
                                                       scalar=const_g[:, 4 * j + t:4 * j + t + 1], in1=conv_u[r][:],
                                                       op0=ALU.mult, op1=ALU.add).then_inc(taps, 1)

                def silu(g, j, p):
                    dve.wait_ge(tanh_done, post_n(q, g + 1, j))
                    dst = xT[p][:, j, :] if j < XT else (BT, CT)[j - XT][p][:]
                    nc.vector.scalar_tensor_tensor(out=dst, in0=conv_in[j % 2][:, 0:TB], scalar=1.0, in1=conv_u[j % 2][:],
                                                   op0=ALU.add, op1=ALU.mult).then_inc(post, 1)

                def gate_tile(g, j, first):
                    if j == 0 and not first:
                        dve.wait_ge(z_done, chunk(q, g - 1, 3) * 2 + (1 + 4))
                    dve.wait_ge(evac_act, act_n(q, g, j))
                    nc.vector.scalar_tensor_tensor(out=gate[:, j, :], in0=conv_in[j % 2][:, 0:TB], scalar=1.0,
                                                   in1=conv_u[j % 2][:], op0=ALU.add, op1=ALU.mult).then_inc(gate_done, 1)

                def chunk_1(g, c):
                    n = chunk(q, g, c)
                    if c == 0:
                        dve.wait_ge(prep_done, q * 9 + g + 2)
                    dve.wait_ge(ck_evac, n * 2 + 1)
                    nc.vector.tensor_tensor(heads(dtx[:]), heads(x_ck[:]), per_head(0, c), ALU.mult).then_inc(xw_done, 1)
                    nc.vector.tensor_tensor(heads(wx[:]), heads(x_ck[:]), per_head(1, c), ALU.mult).then_inc(xw_done, 1)
                    dve.wait_ge(ck_evac, n * 2 + 2)
                    nc.vector.tensor_tensor(CBm[:], pCB[:, N:N + Q], causal[:], ALU.mult).then_inc(cbm_done, 1)
                    dve.wait_ge(cbm_done, n + 1)
                    for h in range(2):
                        dve.wait_ge(exp_done, n * 2 + (h + 1))
                        nc.vector.tensor_tensor(E[:, 4 * h:4 * h + 4, :], E[:, 4 * h:4 * h + 4, :],
                                                CBm[:].unsqueeze(1).broadcast_to([128, 4, Q]), ALU.mult).then_inc(m_done, 1)

                def chunk_2(g, c):
                    n = chunk(q, g, c)
                    dve.wait_ge(s2, n * 2 + 1)
                    nc.vector.tensor_tensor(heads(y[:]), heads(pS[:]), per_head(2, c), ALU.mult).then_inc(y_step, 1)
                    dve.wait_ge(s2, n * 2 + 2)
                    dve.wait_ge(y_step, n * 3 + (1 + CR_2))
                    nc.vector.tensor_tensor(y[:], y[:], pY[:], ALU.add).then_inc(y_step, 1)
                    dve.wait_ge(xd_done, n + 1 + 1)
                    dve.wait_ge(y_step, n * 3 + (2 + CR_2))
                    nc.vector.tensor_tensor(y[:], y[:], xD[:], ALU.add).then_inc(y_step, 1)

                def normalize(g, c):
                    n = chunk(q, g, c)
                    dve.wait_ge(rstd_done, n * 2 + 2)
                    nc.vector.tensor_scalar(yn[c % 2][:], y[:], rstd[:, 1:2], None, ALU.mult).then_inc(yn_done, 1)

                def state(g, c):
                    n = chunk(q, g, c)
                    dve.wait_ge(sdec_done, n + 1)
                    dve.wait_ge(st_done, n + 1)
                    nc.vector.tensor_tensor(S_cur[:], S_dec[:], pS[:], ALU.add).then_inc(s_upd, 1)

                def gated(g, c):
                    n = chunk(q, g, c)
                    if c == 0:
                        dve.wait_ge(gate_done, grp(q, g) * XT + XT)
                    dve.wait_ge(s3, n + 1)
                    nc.vector.tensor_tensor(z_t[:], pX[:].rearrange("p (j t) -> p j t", j=XT),
                                            gate[:, :, c * Q:(c + 1) * Q], ALU.mult).then_inc(z_done, 1)

                def gated_lo(g, c):
                    n = chunk(q, g, c)
                    dve.wait_ge(zhi_done, n + 1)
                    cs = slice(c * Q, (c + 1) * Q)
                    nc.vector.tensor_tensor(z_lo[:, :, cs], z_t[:], z_hi[:, :, cs].bitcast(F32), ALU.subtract)\
                        .then_inc(z_done, 1)

                def out_adds(g, m, tail=False):
                    for h in range(2):
                        i = 2 * m + h
                        dve.wait_ge(dense_done, dense_n(q, g, (K_TAIL if tail else K_OUT) + m, h))
                        n = tail_n(q, i) if tail else out_n(q, g, i)
                        dve.wait_ge(evac_dve, n - 2)
                        b = ((K_TAIL if tail else 3) + i) % 2
                        nc.vector.tensor_tensor(acc[:, i, :], acc[:, i, :], bank[b][:], ALU.add).then_inc(evac_dve, 1)

                def ffn_evac(j):
                    b = (K_X + j) % 2
                    dve.wait_ge(dense_done, dense_n(q, 7, K_X + j, 1))
                    dve.wait_ge(evac_dve, ffn_n(q, j - 2))
                    if j == 0:
                        dve.wait_ge(w_tok_ready, q + 1)
                        nc.vector.tensor_tensor(w_tok[:], w_tok[:], bank[b][:], ALU.mult).then_inc(evac_dve, 1)
                    else:
                        nc.vector.scalar_tensor_tensor(out=acc[:, j - 1, :], in0=bank[b][:], scalar=bb[:, j - 1:j],
                                                       in1=acc[:, j - 1, :], op0=ALU.add, op1=ALU.add).then_inc(evac_dve, 1)

                def prep(g):
                    nc.vector.tensor_scalar(tok_g[:], tok[:, :, bass.ds(g * HPG, HPG)], 1.0, None, ALU.mult)
                    nc.vector.tensor_scalar(D_g[:], D_all[:, bass.ds(g * HPG, HPG)], 1.0, None, ALU.mult)
                    nc.vector.tensor_scalar(const_g[:], consts[:, bass.ds(g + 1, 1), :].rearrange("p a c -> p (a c)"),
                                            1.0, None, ALU.mult)
                    nc.vector.tensor_scalar(halo[:, bass.ds(g, 1), :, :].rearrange("p a j t -> p (a j t)"),
                                            halo_out[:].rearrange("p j t -> p (j t)"), 1.0, None, ALU.mult)
                    nc.vector.tensor_scalar(halo_in[:].rearrange("p j t -> p (j t)"),
                                            halo[:, bass.ds(g + 1, 1), :, :].rearrange("p a j t -> p (a j t)"),
                                            1.0, None, ALU.mult).then_inc(prep_done, 1)
                    dve.wait_ge(s_upd, grp(q, g) * 6 + 1)
                    nc.vector.tensor_scalar(S_cur[:], S_all[:, bass.ds(g, 1), :].rearrange("p a c -> p (a c)"),
                                            1.0, None, ALU.mult).then_inc(s_upd, 1)

                def save_state(g):
                    dve.wait_ge(s_upd, grp(q, g) * 6 + (5 + 1))
                    nc.vector.tensor_scalar(S_all[:, bass.ds(g, 1), :].rearrange("p a c -> p (a c)"), S_cur[:],
                                            1.0, None, ALU.mult).then_inc(s_upd, 1)

                def ln_stats(i):
                    n = (q * NC + i) * 4
                    dve.wait_ge(x_loaded[i % 2], (q * 2 + (i // 2 + 1)) * 16)
                    for h in range(2):
                        nc.vector.bn_stats(stats[:, i, h, :], x_in[i % 2][:, 512 * h:512 * h + 512]).then_inc(ln_stat, 1)
                    dve.wait_ge(ln_stat, n + 2)
                    nc.vector.tensor_tensor(ln_sync[:, i:i + 1], stats[:, i, 0, 1:2], stats[:, i, 1, 1:2], ALU.add).then_inc(ln_stat, 1)
                    nc.vector.bn_aggr(mv[:, i, :], stats[:, i, :, :].rearrange("p a b -> p (a b)")).then_inc(ln_stat, 1)

                def ln_apply(i):
                    if i >= 2:
                        dve.wait_ge(lnT_done, q * (2 * NC) + (2 * (i - 2) + 2))
                    dve.wait_ge(ln_rstd, (q * NC + i) * 2 + 2)
                    nc.vector.tensor_scalar(xn[i % 2], x_in[i % 2][:], mv[:, i, 0:1], ln_r[:, i, 1:2],
                                            ALU.subtract, ALU.mult).then_inc(xn_done, 1)

                def ln_low(i):
                    for h in range(2):
                        dve.wait_ge(xn_hi_done, q * (2 * NC) + (2 * i + h + 1))
                        cols = slice(i * 128, (i + 1) * 128)
                        nc.vector.tensor_tensor(xn_lo[:, 4 * h:4 * h + 4, cols],
                                                ln_banks[(2 * i + h) % 4][:].rearrange("p (k t) -> p k t", k=4),
                                                xn_hi[:, 4 * h:4 * h + 4, cols].bitcast(F32), ALU.subtract)\
                            .then_inc(xn_lo_done, 1)

                ln_stats(0)
                ln_stats(1)
                ln_apply(0)
                ln_apply(1)
                ln_stats(2)
                ln_stats(3)
                ln_low(0)
                ln_apply(2)
                ln_low(1)
                ln_apply(3)
                ln_low(2)
                ln_low(3)
                nc.vector.tensor_copy(const_g[:], consts[:, 0, :])
                nc.vector.tensor_copy(halo_in[:], halo[:, 0, :, :]).then_inc(prep_done, 1)
                lo(0, K_DT)
                dve.wait_ge(dt_act, q * DT_ACT + 2)
                dt_step(nc.vector.tensor_scalar(t_p, t_e, 2.0, None, ALU.add))
                dt_step(nc.vector.reciprocal(t_r, t_p))
                dt_step(nc.vector.tensor_tensor(t_z, t_e, t_r, ALU.mult))
                dt_step(nc.vector.tensor_tensor(t_z2, t_z, t_z, ALU.mult))
                dt_step(nc.vector.tensor_scalar(t_p, t_z2, 1.0 / 15, None, ALU.mult))
                for d in (13, 11, 9, 7, 5, 3):
                    dt_step(nc.vector.scalar_tensor_tensor(out=t_p, in0=t_p, scalar=1.0 / d, in1=t_z2, op0=ALU.add,
                                                           op1=ALU.mult))
                dt_step(nc.vector.scalar_tensor_tensor(out=t_p, in0=t_p, scalar=1.0, in1=t_z, op0=ALU.add, op1=ALU.mult))
                lo(0, K_FIRST)
                dt_step(nc.vector.tensor_scalar(t_v, t_v, 0.0, None, ALU.max))
                dt_step(nc.vector.scalar_tensor_tensor(out=t_dt, in0=t_p, scalar=2.0, in1=t_v, op0=ALU.mult, op1=ALU.add))
                dt_step(nc.vector.tensor_scalar(t_a, t_dt, A_neg[:], LOG_ZERO, ALU.mult, ALU.max))
                for c in range(NC):
                    ins = nc.vector.tensor_tensor_scan(t_cum[:, c * Q:(c + 1) * Q], ones[0:H, :], t_a[:, c * Q:(c + 1) * Q],
                                                       0.0, ALU.mult, ALU.add)
                    if c >= 1:
                        dt_step(ins, wait=False)
                dve.wait_ge(prep_done, q * 9 + 1)
                conv_taps(NO_GROUP, 0)
                lo(0, K_FIRST + 1)
                conv_taps(NO_GROUP, 1)
                silu(-1, 0, 0)
                dve.wait_ge(dt_act, q * DT_ACT + 3)
                dt_step(nc.vector.tensor_tensor(cum_lo[:], t_cum, cum_hi[:].bitcast(F32), ALU.subtract), wait=False)
                dve.wait_ge(dt_act, q * DT_ACT + 8)
                dt_step(nc.vector.tensor_tensor(t_z, t_e, t_dt, ALU.mult), wait=False)
                last_ecum = t_ecum.rearrange("p (c t) -> p c t", c=NC)[:, :, Q - 1:Q].broadcast_to([H, NC, H])
                dt_step(nc.vector.tensor_tensor(t_diag, ident[0:H, 0:H].unsqueeze(1).broadcast_to([H, NC, H]), last_ecum,
                                                ALU.mult), wait=False)
                lo(0, K_FIRST + 2)
                conv_taps(NO_GROUP, 2)
                silu(-1, 1, 0)
                lg = pY[:, 0:NC * NE].rearrange("p (i e) -> p i e", i=NC)
                for i in range(NC):
                    rt_step(nc.vector.max(m8[:, i, :], lg[:, i, :]), wait=i == NC - 1)
                rt_step(nc.vector.tensor_tensor(pr[:, 0, :], m8[:, :, 1], m8[:, :, 0], ALU.subtract), wait=False)
                for i in range(NC):
                    rt_step(nc.vector.max_index(ix8[:, i, :], m8[:, i, :], lg[:, i, :]), wait=i == NC - 1)
                rt_step(nc.vector.tensor_copy(ixf[:], ix8[:, :, 0:2]), wait=False)
                lo(0, K_FIRST + 3)
                conv_taps(NO_GROUP, 3)
                silu(-1, 2, 0)
                dve.wait_ge(dt_act, q * DT_ACT + 9)
                dve.wait_ge(rt_dve, q * RT_DVE + 10)
                rt_step(nc.vector.tensor_scalar(pr[:, 2, :], pr[:, 1, :], 1.0, 0.5, ALU.add, ALU.mult))
                rt_step(nc.vector.reciprocal(pr[:, 2, :], pr[:, 2, :]))
                rt_step(nc.vector.tensor_tensor(pr[:, 3, :], pr[:, 1, :], pr[:, 2, :], ALU.mult))
                for i in range(NC):
                    for s in range(2):
                        ins = nc.vector.tensor_scalar(rw[:, s, i, :], iota[:], ixf[:, i, s:s + 1], pr[:, 2 + s, i:i + 1],
                                                      ALU.is_equal, ALU.mult)
                    if i < NC - 1:
                        rt_step(ins, wait=False)
                rt_step(ins)
                rt_step(nc.vector.tensor_tensor(rw[:, 2], rw[:, 0], rw[:, 1], ALU.add))
                rt_step(nc.vector.tensor_copy(dtx[:].rearrange("t (e r) -> t e r", r=RANK),
                                              rw[:, 2].rearrange("p i e -> p (i e)").unsqueeze(2)
                                              .broadcast_to([128, NC * NE, RANK])), wait=False)
                lo(0, K_FIRST + 4)
                conv_taps(NO_GROUP, 4)
                silu(-1, 3, 0)
                lo(0, K_FIRST + 5)
                conv_taps(NO_GROUP, 5)
                silu(-1, 4, 0)
                silu(-1, 5, 0)
                dve.wait_ge(tok_ready, (q + 1) * 2)
                prep(0)
                assert (n_dt, n_rt) == (DT_DVE, RT_DVE), (n_dt, n_rt)

                def group(g, p, first=False, last=False):
                    def out_unit(m):
                        if not first:
                            lo(g, K_OUT + m)
                            if m == 0:
                                dve.wait_ge(acc_loaded, (q + 1) * 16)
                            out_adds(g, m)

                    def x_unit(j):
                        lo(g, K_X + j)
                        if last:
                            ffn_evac(j)
                        else:
                            conv_taps(g, j)
                            if j >= 1:
                                silu(g, j - 1, 1 - p)

                    lo(g, k_gate(first, 0))
                    lo(g, k_gate(first, 1))
                    chunk_1(g, 0)
                    lo(g, k_gate(first, 2))
                    if not first:
                        gated(g - 1, 3)
                    gate_tile(g, 0, first)
                    gate_tile(g, 1, first)
                    if not first:
                        gated_lo(g - 1, 3)
                    gate_tile(g, 2, first)
                    lo(g, k_gate(first, 3))
                    chunk_2(g, 0)
                    gate_tile(g, 3, first)
                    out_unit(0)
                    normalize(g, 0)
                    state(g, 0)
                    chunk_1(g, 1)
                    out_unit(1)
                    out_unit(2)
                    chunk_2(g, 1)
                    gated(g, 0)
                    out_unit(3)
                    normalize(g, 1)
                    state(g, 1)
                    gated_lo(g, 0)
                    chunk_1(g, 2)
                    x = [3, 4, 6] if last else [2, 3, 5]
                    for j in range(x[0]):
                        x_unit(j)
                    chunk_2(g, 2)
                    gated(g, 1)
                    gated_lo(g, 1)
                    x_unit(x[0])
                    normalize(g, 2)
                    state(g, 2)
                    chunk_1(g, 3)
                    for j in range(x[1], x[2]):
                        x_unit(j)
                    chunk_2(g, 3)
                    gated(g, 2)
                    gated_lo(g, 2)
                    x_unit(x[2])
                    normalize(g, 3)
                    state(g, 3)
                    save_state(g)
                    if last:
                        x_unit(7)
                        x_unit(8)
                    else:
                        silu(g, 5, 1 - p)
                        prep(g + 1)

                group(0, 0, first=True)
                with dve.Fori(0, 3) as pair:
                    group(pair * 2 + 1, 1)
                    group(pair * 2 + 2, 0)
                group(7, 1, last=True)
                gated(7, 3)
                gated_lo(7, 3)
                for m in range(4):
                    lo(7, K_TAIL + m)
                    out_adds(7, m, tail=True)

            with dve.Fori(0, NQ) as q:
                block_body(q)


def _tile_slot(np, rows):
    return np.ascontiguousarray(rows.reshape(128, KD, 128).transpose(2, 1, 0)).reshape(128, KD * 128)


def _pack_weights(np, w_in, w_router, w_out, w_base, lora_a):
    gate_r, x_r, b_r, c_r, dt_r = 0, I, 2 * I, 2 * I + G * N, 2 * I + 2 * G * N
    dt_rows = np.zeros((128, DM), w_in.dtype)
    dt_rows[:H] = w_in[dt_r:dt_r + H]
    dt_rows[H:H + NE] = w_router
    slots = [_tile_slot(np, dt_rows)]

    def conv_set(g):
        for j in range(XT):
            r = x_r + g * GC + j * 128
            slots.append(_tile_slot(np, w_in[r:r + 128]))
        for base in (b_r, c_r):
            slots.append(_tile_slot(np, w_in[base + g * N:base + (g + 1) * N]))

    def out_set(g):
        for m in range(OT // 2):
            part = w_out[m * 256:(m + 1) * 256, g * GC:(g + 1) * GC].reshape(2, 128, KZ, 128)
            slots.append(np.ascontiguousarray(part.transpose(3, 0, 2, 1)).reshape(128, 1024))

    conv_set(0)
    for g in range(G):
        for j in range(XT):
            r = gate_r + g * GC + j * 128
            slots.append(_tile_slot(np, w_in[r:r + 128]))
        if g >= 1:
            out_set(g - 1)
        if g < G - 1:
            conv_set(g + 1)
        else:
            slots.append(_tile_slot(np, lora_a.reshape(NE * RANK, DM)))
            for o in range(OT):
                slots.append(_tile_slot(np, w_base[o * 128:(o + 1) * 128]))
    out_set(G - 1)
    assert len(slots) == SLOTS
    return np.stack(slots + slots[:2])


def _pack_group_consts(np, conv_w, conv_b, norm_w):
    out = np.zeros((128, G + 1, NCONST), conv_w.dtype)
    for g in range(G):
        starts = [g * GC + j * 128 for j in range(XT)] + [I + g * N, I + G * N + g * N]
        for j, r in enumerate(starts):
            out[:, g, 4 * j:4 * j + 4] = conv_w[r:r + 128]
            out[:, g, 4 * NSET + j] = conv_b[r:r + 128]
        for j in range(XT):
            out[:, g + 1, 5 * NSET + j] = norm_w[g * GC + j * 128:g * GC + (j + 1) * 128]
    return out


def kernel(**inputs):
    import numpy as np
    import concourse.bacc as bacc
    from concourse.bass_utils import run_bass_kernel_spmd as run

    a = {k: np.ascontiguousarray(v) for k, v in inputs.items()}
    x = a["L0_attn_hidden_states"].reshape(L, DM)
    arrays = {
        "x_tok_dram": x,
        "x_tr_dram": np.ascontiguousarray(x.T),
        "w_slots_dram": _pack_weights(np, a["L0_attn_in_proj_w"], a["L0_ffn_W_router"], a["L0_attn_out_proj_w"],
                                      a["L0_ffn_W_base"], a["L0_ffn_A"]),
        "group_const_dram": _pack_group_consts(np, a["L0_attn_conv_weight"], a["L0_attn_conv_bias"],
                                               a["L0_attn_norm_weight"]),
        "dt_bias_dram": a["L0_attn_dt_bias"].reshape(H, 1),
        "a_log_dram": a["L0_attn_A_log"].reshape(H, 1),
        "d_skip_dram": np.ascontiguousarray(np.broadcast_to(a["L0_attn_D"], (128, H))),
        "b_base_dram": np.ascontiguousarray(a["L0_ffn_b_base"].reshape(OT, 128).T),
        "lora_b_dram": np.ascontiguousarray(a["L0_ffn_B"].transpose(0, 2, 1)).reshape(NE * RANK, DM),
    }
    nc = bacc.Bacc("TRN2", target_bir_lowering=False, num_devices=1)
    args = [nc.dram_tensor(n, v.shape, mybir.dt.from_np(v.dtype), kind="ExternalInput").ap() for n, v in arrays.items()]
    args.append(nc.dram_tensor("out_tr_dram", (DM, L), F32, kind="ExternalOutput").ap())
    layer_kernel(nc, *args)
    r = run(nc, [arrays], core_ids=[0])
    out = r.results[0]["out_tr_dram"]
    return np.ascontiguousarray(out.T).reshape(1, L, DM)
```

```python
import concourse.bass as bass
from concourse import mybir
from contextlib import ExitStack

F32 = mybir.dt.float32
F32R = mybir.dt.float32r
U32 = mybir.dt.uint32
ALU = mybir.AluOpType
ACT = mybir.ActivationFunctionType

L, DM, H, P, N, G = 2048, 1024, 64, 64, 128, 8
I = H * P
HPG = H // G
GC = I // G
TB = 512
NQ = L // TB
Q = 128
NC = TB // Q
KD = DM // 128
XT = GC // 128
NSET = XT + 2
KZ = GC // 128
OT = DM // 128
NE, RANK = 8, 16
EPS = 1e-5
LOG_ZERO = -104.0
NCONST = NSET * 4 + NSET + XT
BIAS0, NORM0 = 4 * NSET, 5 * NSET

PER_G = 14
SLOTS = 1 + NSET + 10 + 6 * PER_G + 17 + 4
K_DT, K_FIRST = 0, 1
K_X = 11
K_OUT = 7
K_TAIL = 20


def k_gate(g_is_0, j):
    return (7 if g_is_0 else 3) + j


NO_GROUP = -1

ACT_EV = 1 + NSET + G * XT + (G - 1) * NSET
DVE_EV = (G - 1) * OT + (1 + OT) + OT
PREPS = G + 1
S_STEPS = NC + 2
LN_STEPS = 4

CR_DENSE, CR_EVAC, CR_2 = 4, 2, 2


def layer_kernel(nc, x_tok, x_tr, w_slots, group_const, dt_bias, a_log, d_skip, b_base, lora_b, out_tr):
    ctx = ExitStack()
    with ctx:
        def sb(name, shape, dt=F32):
            return ctx.enter_context(nc.sbuf_tensor(name, shape, dt))

        def pb(name):
            return ctx.enter_context(nc.psum_tensor(name, [128, 512], F32))

        def sem(name):
            return ctx.enter_context(nc.semaphore(name))

        xn_hi = sb("xn_hi", [128, KD, TB], F32R)
        xn_lo = sb("xn_lo", [128, KD, TB], F32R)
        w_raw = [sb(f"w_raw{i}", [128, 1024]) for i in range(2)]
        w_hi = [sb(f"w_hi{i}", [128, 1024], F32R) for i in range(2)]
        w_lo = [sb(f"w_lo{i}", [128, 1024], F32R) for i in range(2)]
        xT = [sb(f"xT{i}", [128, XT, TB]) for i in range(2)]
        BC = [sb(f"BC{i}", [128, 2, TB]) for i in range(2)]
        BT, CT = ([bc[:, i, :] for bc in BC] for i in range(2))
        gate = sb("gate", [128, XT, TB])
        conv_in = [sb(f"conv_in{i}", [128, TB + 3]) for i in range(2)]
        conv_us = sb("conv_us", [128, 2, TB])
        conv_u = [conv_us[:, i, :] for i in range(2)]
        S_all = sb("S_all", [128, G, GC])
        S_cur = sb("S_cur", [128, GC])
        S_dec = sb("S_dec", [128, GC])
        acc = sb("acc", [128, OT, TB])
        z_hi = sb("z_hi", [128, XT, TB], F32R)
        z_lo = sb("z_lo", [128, XT, TB], F32R)
        z_t = sb("z_t", [128, XT, Q])
        x_ck = sb("x_ck", [128, GC])
        B_hi, B_lo = sb("B_hi", [128, N], F32R), sb("B_lo", [128, N], F32R)
        C_hi, C_lo = sb("C_hi", [128, Q], F32R), sb("C_lo", [128, Q], F32R)
        S_hi, S_lo = sb("S_hi", [128, GC], F32R), sb("S_lo", [128, GC], F32R)
        wx_hi, wx_lo = sb("wx_hi", [128, GC], F32R), sb("wx_lo", [128, GC], F32R)
        CBm = sb("CBm", [128, Q])
        E = sb("E", [128, HPG, Q])
        dtx = sb("dtx", [128, GC])
        wx = sb("wx", [128, GC])
        xD = sb("xD", [128, GC])
        y = sb("y", [128, GC])
        yn = [sb(f"yn{i}", [128, GC]) for i in range(2)]
        ssq = sb("ssq", [128, 1])
        rstd = sb("rstd", [128, 2])
        cum_b = [sb(f"cum_b{i}", [128, HPG, Q]) for i in range(2)]
        w_tok = sb("w_tok", [128, TB])
        lora_sb = sb("lora_sb", [128, DM])
        tok = sb("tok", [128, 5 * NC, H])
        tok_g = sb("tok_g", [128, 5 * NC, HPG])
        D_all = sb("D_all", [128, H])
        D_g = sb("D_g", [128, HPG])
        consts = sb("consts", [128, G + 1, NCONST])
        const_g = sb("const_g", [128, NCONST])
        halo = sb("halo", [128, G + 1, NSET, 3])
        halo_in = sb("halo_in", [128, NSET, 3])
        halo_out = sb("halo_out", [128, NSET, 3])
        x_next = [t[:].rearrange("p a b -> p (a b)") for t in (BC[0], conv_us)] * 2
        ident = sb("ident", [128, 128])
        causal = sb("causal", [128, 128])
        ones = sb("ones", [128, 128])
        iota = sb("iota", [128, NE])
        eps_t = sb("eps_t", [128, 2])
        dtb = sb("dtb", [128, H])
        A_neg = sb("A_neg", [128, H])
        bb = sb("bb", [128, OT])
        stats = sb("stats", [128, NC, 2, 6])
        ln_sync = sb("ln_sync", [128, NC])
        mv = sb("mv", [128, NC, 2])
        ln_r = sb("ln_r", [128, NC, 2])
        m8 = sb("m8", [128, NC, 8])
        ix8 = sb("ix8", [128, NC, 8], U32)
        ixf = sb("ixf", [128, NC, 2])
        pr = sb("pr", [128, 4, NC])
        rw = sb("rw", [128, 3, NC, NE])
        t_v, t_e, t_p, t_r, t_z, t_z2, t_a = (t[:, 0:NC * H] for t in (dtx, wx, xD, y, yn[0], yn[1], x_ck))
        t_diff = x_ck[:, NC * H:2 * NC * H]
        tk_dt, tk_w, tk_ecum, tk_elast, tk_cum = (tok[:, NC * i:NC * (i + 1), :].rearrange("p c h -> p (c h)")
                                                  for i in range(5))
        t_cumT = z_t[0:H].rearrange("p j t -> p (j t)")
        E_flat = E[:].rearrange("p h t -> p (h t)")
        dtT = xT[0][:, XT - 1, :]

        def token_tiles(t):
            return [t[:, 2 * i:2 * i + 2, :].rearrange("p a b -> p (a b)") for i in range(t.shape[1] // 2)]

        xn_next = token_tiles(xT[0]) * 2
        x_first, xn_first = token_tiles(acc), token_tiles(xT[0]) + token_tiles(gate)
        cum_dram = nc.dram_tensor("cum_scratch", [NC, H, Q], F32).ap()

        bank = [pb("dense0"), pb("dense1")]
        pX, pCB, pD0, pD1, pY, pS = pb("pX"), pb("pCB"), pb("pD0"), pb("pD1"), pb("pY"), pb("pS")
        ln_banks = [pCB, pX, pD1, pY]
        ln_banks_first = ln_banks + [pD0, pS] + bank

        const_loaded = sem("const_loaded")
        const_made = sem("const_made")
        zeroed = sem("zeroed")
        const_vec = sem("const_vec")
        const_act = sem("const_act")
        w_loaded = [sem("w_loaded0"), sem("w_loaded1")]
        hi_done = sem("hi_done")
        lo0_done = sem("lo0_done")
        lo1_done = sem("lo1_done")
        dense_done = sem("dense_done")
        evac_act = sem("evac_act")
        evac_dve = sem("evac_dve")
        x_loaded = [sem(f"x_loaded{i}") for i in range(NC)]
        ln_stat = sem("ln_stat")
        ln_rstd = sem("ln_rstd")
        xn_done = sem("xn_done")
        lnT_done = sem("lnT_done")
        xn_hi_done = sem("xn_hi_done")
        xn_lo_done = sem("xn_lo_done")
        dt_act = sem("dt_act")
        dt_dve = sem("dt_dve")
        rt_dve = sem("rt_dve")
        rt_act = sem("rt_act")
        cum_done = sem("cum_done")
        cumT_done = sem("cumT_done")
        lg_done = sem("lg_done")
        wT_done = sem("wT_done")
        w_tok_ready = sem("w_tok_ready")
        cum_stored = sem("cum_stored")
        cumb_loaded = [sem("cumb_loaded0"), sem("cumb_loaded1")]
        acc_loaded = sem("acc_loaded")
        out_stored = sem("out_stored")
        prep_done = sem("prep_done")
        taps = sem("taps")
        tanh_done = sem("tanh_done")
        post = sem("post")
        gate_done = sem("gate_done")
        s1 = sem("s1")
        ck_evac = sem("ck_evac")
        relu_done = sem("relu_done")
        exp_done = sem("exp_done")
        cbm_done = sem("cbm_done")
        bl_done = sem("bl_done")
        m_done = sem("m_done")
        xw_done = sem("xw_done")
        cs_hi = sem("cs_hi")
        cs_lo = sem("cs_lo")
        wx_hi_done = sem("wx_hi_done")
        wx_lo_done = sem("wx_lo_done")
        xd_done = sem("xd_done")
        sdec_done = sem("sdec_done")
        s_upd = sem("s_upd")
        s2 = sem("s2")
        st_done = sem("st_done")
        y_step = sem("y_step")
        sq_done = sem("sq_done")
        rstd_done = sem("rstd_done")
        yn_done = sem("yn_done")
        s3 = sem("s3")
        z_done = sem("z_done")
        zhi_done = sem("zhi_done")

        def slot(q, g, k):
            return q * SLOTS + g * PER_G + k

        def dense_n(q, g, k, h):
            return q * (2 * SLOTS) + g * (2 * PER_G) + (2 * k + h + 1 + CR_DENSE)

        def act_n(q, g, j):
            return q * ACT_EV + g * (XT + NSET) + (1 + NSET + j + 1 + CR_EVAC)

        def out_n(q, g, i):
            return q * DVE_EV + g * OT + (i - OT + 1 + CR_EVAC)

        def ffn_n(q, j):
            return q * DVE_EV + ((G - 1) * OT + j + 1 + CR_EVAC)

        def tail_n(q, i):
            return q * DVE_EV + (G * OT + 1 + i + 1 + CR_EVAC)

        def grp(q, g):
            return q * G + g

        def chunk(q, g, c):
            return q * (G * NC) + g * NC + c

        def post_n(q, g, j):
            return q * (G * NSET) + g * NSET + (j + 1)

        DT_ACT, DT_DVE, RT_DVE = 7, 19, 19

        block = ctx.enter_context(nc.Block())

        @block.sync
        def _(sp):
            def load_x(b, i, dst):
                sp.dma_start(dst[i], x_tok[bass.ds(b * TB + i * 128, 128), :]).then_inc(x_loaded[i], 16)

            load_x(0, 0, x_first)
            load_x(0, 1, x_first)
            sp.dma_start(w_raw[0][:], w_slots[0]).then_inc(w_loaded[0], 16)
            load_x(0, 2, x_first)
            load_x(0, 3, x_first)
            sp.dma_start(w_raw[1][:], w_slots[1]).then_inc(w_loaded[1], 16)
            for t, src in ((consts, group_const), (D_all, d_skip), (bb, b_base), (lora_sb, lora_b),
                           (dtb, dt_bias), (A_neg, a_log)):
                sp.dma_start(t[:], src).then_inc(const_loaded, 16)
            with sp.Fori(0, NQ) as q:
                def load_w(n, s):
                    sp.wait_ge(lo0_done, q * SLOTS + n - 1)
                    sp.wait_ge(lo1_done, q * SLOTS + n - 1)
                    sp.dma_start(w_raw[s][:], w_slots[n]).then_inc(w_loaded[s], 16)

                def load_pairs(first, end):
                    with sp.Fori(first, end) as pair:
                        for s in range(2):
                            sp.wait_ge(lo0_done, q * SLOTS + pair * 2 + (s - 1))
                            sp.wait_ge(lo1_done, q * SLOTS + pair * 2 + (s - 1))
                            sp.dma_start(w_raw[s][:], w_slots[bass.ds(pair * 2 + s, 1)].rearrange("o p f -> (o p) f"))\
                              .then_inc(w_loaded[s], 16)

                load_w(2, 0)
                load_w(3, 1)
                load_pairs(2, SLOTS // 2 - 7)
                sp.wait_ge(s2, chunk(q, 6, 3) * 2 + 2)
                sp.wait_ge(gate_done, grp(q, 7) * XT + XT)
                load_x(q + 1, 0, x_next)
                load_x(q + 1, 1, x_next)
                load_pairs(SLOTS // 2 - 7, SLOTS // 2 - 2)
                sp.wait_ge(xn_done, q * NC + (NC + 1 + CR_2))
                load_x(q + 1, 2, x_next)
                sp.wait_ge(xn_done, q * NC + (NC + 2 + CR_2))
                load_x(q + 1, 3, x_next)
                load_pairs(SLOTS // 2 - 2, SLOTS // 2 + 1)
            sp.wait_ge(out_stored, 16 + NQ * 64)

        @block.gpsimd
        def _(pool):
            pool.sem_inc(xd_done, 1)
            n_made = 0

            def made(ins):
                nonlocal n_made
                n_made += 1
                ins.then_inc(const_made, 1)

            made(nc.gpsimd.memset(ident[:], 0.0))
            made(nc.gpsimd.memset(causal[:], 1.0))
            made(nc.gpsimd.memset(ones[:], 1.0))
            made(nc.gpsimd.memset(eps_t[:, 0:1], EPS))
            made(nc.gpsimd.memset(eps_t[:, 1:2], -0.5))
            for e in range(NE):
                made(nc.gpsimd.memset(iota[:, e:e + 1], float(e)))
            pool.wait_ge(const_made, n_made)
            made(nc.gpsimd.affine_select(out=ident[:], in_=ident[:], compare_op=ALU.not_equal, fill=1.0, base=0,
                                         pattern=[[-1, 128]], channel_multiplier=1))
            made(nc.gpsimd.affine_select(out=causal[:], in_=causal[:], compare_op=ALU.is_ge, fill=0.0, base=0,
                                         pattern=[[1, 128]], channel_multiplier=-1))
            assert n_made == 15

            def lo_first_half(s, n):
                pool.wait_ge(hi_done, n)
                nc.gpsimd.tensor_tensor(w_lo[s][:, 0:512], w_raw[s][:, 0:512], w_hi[s][:, 0:512].bitcast(F32),
                                        ALU.subtract).then_inc(lo0_done, 1)

            def ln_inv(b, i):
                n = b * NC + i
                pool.wait_ge(ln_stat, n * LN_STEPS + LN_STEPS)
                nc.gpsimd.tensor_tensor(ln_r[:, i, 0:1], mv[:, i, 1:2], eps_t[:, 0:1], ALU.add).then_inc(ln_rstd, 1)
                pool.wait_ge(ln_rstd, n * 2 + 1)
                nc.gpsimd.tensor_tensor(ln_r[:, i, 1:2], ln_r[:, i, 0:1], eps_t[:, 1:2], ALU.pow).then_inc(ln_rstd, 1)

            ln_inv(0, 0)
            ln_inv(0, 1)
            for s in range(2):
                lo_first_half(s, 2 * s + 1)
            ln_inv(0, 2)
            ln_inv(0, 3)
            for t in (halo, halo_out, S_all):
                nc.gpsimd.memset(t[:], 0.0).then_inc(zeroed, 1)

            def block_body(q):
                def lo(g, k):
                    lo_first_half(k % 2, q * (2 * SLOTS) + g * (2 * PER_G) + (2 * (k + 2) + 1))

                def lo_both(g, k):
                    lo(g, k)
                    pool.wait_ge(hi_done, q * (2 * SLOTS) + g * (2 * PER_G) + (2 * (k + 2) + 2))
                    nc.gpsimd.tensor_tensor(w_lo[k % 2][:, 512:1024], w_raw[k % 2][:, 512:1024],
                                            w_hi[k % 2][:, 512:1024].bitcast(F32), ALU.subtract).then_inc(lo1_done, 1)

                def chunk_pre(g, p, c):
                    n = chunk(q, g, c)
                    if c == 0:
                        pool.wait_ge(prep_done, q * PREPS + g + 2)
                    pool.wait_ge(y_step, n * 3 + CR_2)
                    pool.wait_ge(ck_evac, n * 2 + 1)
                    nc.gpsimd.tensor_tensor(xD[:].rearrange("t (h p) -> t h p", h=HPG),
                                            x_ck[:].rearrange("t (h p) -> t h p", h=HPG),
                                            D_g[:].unsqueeze(2).broadcast_to([128, HPG, P]), ALU.mult)\
                        .then_inc(xd_done, 1)
                    pool.wait_ge(s_upd, grp(q, g) * S_STEPS + (c + 1 + 1))
                    nc.gpsimd.tensor_tensor(S_dec[:].rearrange("n (h p) -> n h p", h=HPG),
                                            S_cur[:].rearrange("n (h p) -> n h p", h=HPG),
                                            tok_g[:, 3 * NC + c, :].unsqueeze(2).broadcast_to([128, HPG, P]), ALU.mult)\
                        .then_inc(sdec_done, 1)
                    pool.wait_ge(cs_hi, n + 1)
                    for lo_part, raw, hi_part in ((C_lo, CT[p][:, c * Q:(c + 1) * Q], C_hi), (S_lo, S_cur[:], S_hi)):
                        ins = nc.gpsimd.tensor_tensor(lo_part[:], raw, hi_part[:].bitcast(F32), ALU.subtract)
                    ins.then_inc(cs_lo, 1)

                def wx_low(g, c):
                    pool.wait_ge(wx_hi_done, chunk(q, g, c) + 1)
                    nc.gpsimd.tensor_tensor(wx_lo[:], wx[:], wx_hi[:].bitcast(F32), ALU.subtract).then_inc(wx_lo_done, 1)

                def inv_rms(g, c):
                    n = chunk(q, g, c)
                    pool.wait_ge(sq_done, n + 1 + 1)
                    nc.gpsimd.tensor_tensor(rstd[:, 0:1], ssq[:], eps_t[:, 0:1], ALU.add).then_inc(rstd_done, 1)
                    pool.wait_ge(rstd_done, n * 2 + 1)
                    nc.gpsimd.tensor_tensor(rstd[:, 1:2], rstd[:, 0:1], eps_t[:, 1:2], ALU.pow).then_inc(rstd_done, 1)

                pool.wait_ge(lo1_done, q * SLOTS + 2)
                lo_both(0, K_DT)
                for j in range(NSET):
                    lo_both(0, K_FIRST + j)

                def group(g, p, first=False, last=False):
                    lo(g, k_gate(first, 0))
                    lo(g, k_gate(first, 1))
                    chunk_pre(g, p, 0)
                    lo(g, k_gate(first, 2))
                    wx_low(g, 0)
                    lo(g, k_gate(first, 3))
                    if not first:
                        lo(g, K_OUT)
                    inv_rms(g, 0)
                    chunk_pre(g, p, 1)
                    if first:
                        lo(g, K_X)
                        wx_low(g, 1)
                        lo(g, K_X + 1)
                    else:
                        lo(g, K_OUT + 1)
                        wx_low(g, 1)
                        lo(g, K_OUT + 2)
                        lo(g, K_OUT + 3)
                    inv_rms(g, 1)
                    chunk_pre(g, p, 2)
                    k = K_X + (2 if first else 0)
                    lo(g, k)
                    wx_low(g, 2)
                    k += 1
                    while k < K_X + (4 if first or last else 3):
                        lo(g, k)
                        k += 1
                    inv_rms(g, 2)
                    chunk_pre(g, p, 3)
                    if last:
                        ln_inv(q + 1, 0)
                        ln_inv(q + 1, 1)
                    lo(g, k)
                    wx_low(g, 3)
                    k += 1
                    while k < K_X + (7 if last else 6):
                        lo(g, k)
                        k += 1
                    inv_rms(g, 3)
                    if last:
                        lo(g, K_X + 7)
                        ln_inv(q + 1, 2)
                        ln_inv(q + 1, 3)
                        lo(g, K_X + 8)

                group(0, 0, first=True)
                with pool.Fori(0, 3) as pair:
                    group(pair * 2 + 1, 1)
                    group(pair * 2 + 2, 0)
                group(7, 1, last=True)
                for m in range(4):
                    lo(7, K_TAIL + m)

            with pool.Fori(0, NQ) as q:
                block_body(q)

        @block.scalar
        def _(act):
            act.sem_inc(evac_act, CR_EVAC)
            act.sem_inc(sq_done, 1)
            act.sem_inc(out_stored, 16)

            def split_hi(s, h):
                sl = slice(512 * h, 512 * h + 512)
                nc.scalar.activation(w_hi[s][:, sl], w_raw[s][:, sl], ACT.Copy).then_inc(hi_done, 1)

            def ln_high(b, i, banks=ln_banks):
                for h in range(2):
                    act.wait_ge(lnT_done, b * (2 * NC) + (2 * i + h + 1))
                    nc.scalar.activation(xn_hi[:, 4 * h:4 * h + 4, i * 128:(i + 1) * 128],
                                         banks[(2 * i + h) % len(banks)][:].rearrange("p (k t) -> p k t", k=4), ACT.Copy)\
                        .then_inc(xn_hi_done, 1)

            for i in range(NC):
                if i < 2:
                    act.wait_ge(w_loaded[i], 16)
                    split_hi(i, 0)
                    split_hi(i, 1)
                ln_high(0, i, ln_banks_first)
            act.wait_ge(const_loaded, 96)
            nc.scalar.activation(A_neg[:], A_neg[:], ACT.Exp).then_inc(const_act, 1)

            def block_body(q):
                n_dt = 0

                def dt_step(ins):
                    nonlocal n_dt
                    n_dt += 1
                    ins.then_inc(dt_act, 1)

                def dt_wait():
                    act.wait_ge(dt_act, q * DT_ACT + n_dt)

                def split(g, k):
                    s = k % 2
                    act.wait_ge(w_loaded[s], (q * (SLOTS // 2) + g * (PER_G // 2) + ((k + 2) // 2 + 1)) * 16)
                    for h in range(2):
                        act.wait_ge(dense_done, dense_n(q, g, k, h))
                        split_hi(s, h)

                def ev_conv(g, k, j, b):
                    r = j % 2
                    act.wait_ge(dense_done, dense_n(q, g if k >= K_X else 0, k, 1))
                    if j >= 2:
                        act.wait_ge(post, post_n(q, g + 1, j - 2))
                    elif k >= K_X:
                        act.wait_ge(gate_done, grp(q, g) * XT + (j + 2 + 1))
                    if j == 0:
                        act.wait_ge(prep_done, q * PREPS + g + 2)
                    nc.scalar.activation(conv_in[r][:, 3:3 + TB], bank[b][:], ACT.Copy)
                    nc.scalar.activation(conv_u[r], bank[b][:], ACT.Identity, bias=const_g[:, BIAS0 + j:BIAS0 + j + 1],
                                         scale=const_g[:, 4 * j + 3:4 * j + 4]).then_inc(evac_act, 1)

                def tanh_conv(g, j):
                    act.wait_ge(taps, (post_n(q, g + 1, j)) * 4)
                    nc.scalar.activation(conv_in[j % 2][:, 0:TB], conv_u[j % 2], ACT.Tanh).then_inc(tanh_done, 1)

                def ev_gate(g, first, j):
                    k = k_gate(first, j)
                    b = (k if first else k - 4) % 2
                    act.wait_ge(dense_done, dense_n(q, g, k, 1))
                    if j < 2:
                        act.wait_ge(post, post_n(q, g, 4 + j))
                    else:
                        act.wait_ge(gate_done, grp(q, g) * XT + (j - 2 + 1))
                    if j == 0:
                        act.wait_ge(prep_done, q * PREPS + g + 2)
                    nc.scalar.activation(conv_in[j % 2][:, 0:TB], bank[b][:], ACT.Tanh, scale=0.5)
                    nc.scalar.activation(conv_u[j % 2], bank[b][:], ACT.Copy,
                                         scale=const_g[:, NORM0 + j:NORM0 + j + 1]).then_inc(evac_act, 1)

                def load_cum(g, c):
                    act.dma_start(cum_b[c % 2][:], cum_dram[c, bass.ds(g * HPG, HPG), :].unsqueeze(0)
                                  .broadcast_to([128, HPG, Q])).then_inc(cumb_loaded[c % 2], 16)

                def chunk_1(g, p, c, last=False):
                    n = chunk(q, g, c)
                    act.wait_ge(xd_done, n + 1)
                    act.wait_ge(s1, n * 2 + 1)
                    nc.scalar.activation(x_ck[:], pX[:], ACT.Copy).then_inc(ck_evac, 1)
                    act.wait_ge(s1, n * 2 + 2)
                    nc.scalar.activation(B_hi[:], pCB[:, 0:N], ACT.Copy).then_inc(ck_evac, 1)
                    nc.scalar.activation(C_hi[:], CT[p][:, c * Q:(c + 1) * Q], ACT.Copy)
                    act.wait_ge(cumb_loaded[c % 2], (q * (2 * G) + g * 2 + (c // 2 + 1)) * 16)
                    for h in range(HPG):
                        ins = nc.scalar.activation(E[:, h, :], cum_b[c % 2][:, h, :], ACT.Relu, scale=-1.0,
                                                   bias=tok_g[:, 4 * NC + c, h:h + 1])
                        if h % 4 == 3:
                            ins.then_inc(relu_done, 1)
                    act.wait_ge(s_upd, grp(q, g) * S_STEPS + (c + 1 + 1))
                    nc.scalar.activation(S_hi[:], S_cur[:], ACT.Copy).then_inc(cs_hi, 1)
                    for h in range(2):
                        act.wait_ge(relu_done, n * 2 + (h + 1))
                        nc.scalar.activation(E_flat[:, 512 * h:512 * h + 512], E_flat[:, 512 * h:512 * h + 512], ACT.Exp,
                                             scale=-1.0).then_inc(exp_done, 1)
                    act.wait_ge(xw_done, n * 2 + 2)
                    nc.scalar.activation(wx_hi[:], wx[:], ACT.Copy).then_inc(wx_hi_done, 1)
                    if c < 2:
                        load_cum(g, c + 2)
                    elif not last:
                        load_cum(g + 1, c - 2)

                def mean_square(g, c):
                    n = chunk(q, g, c)
                    act.wait_ge(y_step, n * 3 + (3 + CR_2))
                    nc.scalar.activation(xD[:], y[:], ACT.Square, scale=float(GC) ** -0.5,
                                         accum_out=ssq[:]).then_inc(sq_done, 1)

                def z_high(g, c):
                    act.wait_ge(z_done, chunk(q, g, c) * 2 + (1 + 4))
                    nc.scalar.activation(z_hi[:, :, c * Q:(c + 1) * Q], z_t[:], ACT.Copy).then_inc(zhi_done, 1)

                split(0, K_DT)
                act.wait_ge(dense_done, dense_n(q, 0, K_DT, 1))
                nc.scalar.activation(dtT, bank[0][:], ACT.Copy).then_inc(evac_act, 1)

                def first_unit(j):
                    split(0, K_FIRST + j)
                    if j >= 1:
                        tanh_conv(-1, j - 1)
                    ev_conv(-1, K_FIRST + j, j, (1 + j) % 2)

                first_unit(0)
                act.wait_ge(dt_dve, q * DT_DVE + 1)
                dt_step(nc.scalar.activation(t_e, t_v, ACT.Abs))
                dt_wait()
                dt_step(nc.scalar.activation(t_e, t_e, ACT.Exp, scale=-1.0))
                first_unit(1)
                first_unit(2)
                first_unit(3)
                act.wait_ge(cum_done, q + 1)
                dt_step(nc.scalar.activation(tk_cum, pY[:, 0:NC * H], ACT.Copy))
                dt_step(nc.scalar.activation(tk_ecum, pY[:, 0:NC * H], ACT.Exp))
                dt_step(nc.scalar.activation(tk_elast, pY[:, NC * H:2 * NC * H], ACT.Exp))
                first_unit(4)
                act.wait_ge(dt_dve, q * DT_DVE + 18)
                dt_step(nc.scalar.activation(t_e, t_diff, ACT.Exp))
                act.wait_ge(cumT_done, q + 1)
                dt_step(nc.scalar.activation(t_cumT, pD1[0:H, :], ACT.Copy))
                dt_wait()
                act.dma_start(cum_dram.rearrange("c h t -> h c t"), t_cumT.rearrange("h (c t) -> h c t", c=NC))\
                    .then_inc(cum_stored, 16)
                first_unit(5)
                act.wait_ge(cum_stored, (q + 1) * 16)
                load_cum(0, 0)
                load_cum(0, 1)
                tanh_conv(-1, 5)
                act.wait_ge(out_stored, q * 64 + 16)
                act.dma_start(acc[:], x_tr[bass.ds(q, 1)].rearrange("b p o t -> (b p) o t"))\
                    .then_inc(acc_loaded, 16)
                assert n_dt == DT_ACT, n_dt

                def router_exp():
                    act.wait_ge(rt_dve, q * RT_DVE + 5)
                    nc.scalar.activation(pr[:, 1, :], pr[:, 0, :], ACT.Exp).then_inc(rt_act, 1)

                def router_copy():
                    act.wait_ge(wT_done, q + 1)
                    nc.scalar.activation(w_tok[:], pD1[:], ACT.Copy).then_inc(w_tok_ready, 1)

                def group(g, p, first=False, last=False):
                    def gate_unit(j):
                        split(g, k_gate(first, j))
                        ev_gate(g, first, j)

                    def x_unit(j):
                        split(g, K_X + j)
                        if not last:
                            if j >= 1:
                                tanh_conv(g, j - 1)
                            ev_conv(g, K_X + j, j, (K_X + j) % 2)

                    def out_unit(m):
                        if not first:
                            split(g, K_OUT + m)

                    gate_unit(0)
                    gate_unit(1)
                    chunk_1(g, p, 0, last)
                    split(g, k_gate(first, 2))
                    if not first:
                        z_high(g - 1, 3)
                    ev_gate(g, first, 2)
                    gate_unit(3)
                    out_unit(0)
                    if first:
                        router_exp()
                    mean_square(g, 0)
                    chunk_1(g, p, 1, last)
                    out_unit(1)
                    out_unit(2)
                    if first:
                        x_unit(0)
                        x_unit(1)
                    out_unit(3)
                    mean_square(g, 1)
                    if not first:
                        act.wait_ge(dense_done, dense_n(q, g, K_OUT + 3, 1))
                    z_high(g, 0)
                    if last:
                        router_copy()
                    chunk_1(g, p, 2, last)
                    x = [2, 4, 4, 6, 6] if first else [0, 3, 4, 6, 7] if last else [0, 2, 3, 5, 6]
                    for j in range(x[0], x[1]):
                        x_unit(j)
                    z_high(g, 1)
                    for j in range(x[1], x[2]):
                        x_unit(j)
                    mean_square(g, 2)
                    chunk_1(g, p, 3, last)
                    for j in range(x[2], x[3]):
                        x_unit(j)
                    z_high(g, 2)
                    for j in range(x[3], x[4]):
                        x_unit(j)
                    mean_square(g, 3)
                    if last:
                        x_unit(7)
                        z_high(7, 3)
                        x_unit(8)
                    else:
                        tanh_conv(g, 5)

                group(0, 0, first=True)
                with act.Fori(0, 3) as pair:
                    group(pair * 2 + 1, 1)
                    group(pair * 2 + 2, 0)
                group(7, 1, last=True)

                def store(m):
                    act.wait_ge(evac_dve, tail_n(q, 2 * m + 1))
                    act.dma_start(out_tr[bass.ds(q, 1), :, 2 * m:2 * m + 2, :].rearrange("b p o t -> (b p) o t"),
                                  acc[:, 2 * m:2 * m + 2, :]).then_inc(out_stored, 16)

                ln_high(q + 1, 0)
                ln_high(q + 1, 1)
                split(7, K_TAIL)
                ln_high(q + 1, 2)
                split(7, K_TAIL + 1)
                store(0)
                ln_high(q + 1, 3)
                split(7, K_TAIL + 2)
                store(1)
                split(7, K_TAIL + 3)
                store(2)
                store(3)

            with act.Fori(0, NQ) as q:
                block_body(q)

        @block.tensor
        def _(pe):
            pe.sem_inc(dense_done, CR_DENSE)
            pe.wait_ge(const_made, 15)

            def ln_transpose(b, i, src=xn_next, banks=ln_banks):
                pe.wait_ge(xn_done, b * NC + (i + 1 + CR_2))
                for h in range(2):
                    if 2 * i + h >= len(banks):
                        pe.wait_ge(xn_lo_done, b * (2 * NC) + (2 * i + h - 4 + 1))
                    for t in range(4):
                        mm = nc.tensor.transpose(banks[(2 * i + h) % len(banks)][:, t * 128:(t + 1) * 128],
                                                 src[i][:, (4 * h + t) * 128:(4 * h + t + 1) * 128], ident[:])
                    mm.then_inc(lnT_done, 1)

            for i in range(NC):
                ln_transpose(0, i, xn_first, ln_banks_first)

            def block_body(q):
                def weights(g, k, h):
                    pe.wait_ge(lo0_done if h == 0 else lo1_done, slot(q, g, k) + 1)

                def w(k, t):
                    return (w_hi[k % 2][:, t * 128:(t + 1) * 128], w_lo[k % 2][:, t * 128:(t + 1) * 128])

                def three(out, lhs, rhs, start, stop):
                    nc.tensor.matmul(out, lhs[0], rhs[0], start=start, stop=False)
                    nc.tensor.matmul(out, lhs[0], rhs[1], start=False, stop=False)
                    return nc.tensor.matmul(out, lhs[1], rhs[0], start=False, stop=stop)

                def in_unit(g, k, b, more=None):
                    for h in range(2):
                        weights(g, k, h)
                        for t in range(4 * h, 4 * h + 4):
                            mm = three(bank[b][:], w(k, t), (xn_hi[:, t, :], xn_lo[:, t, :]), t == 0,
                                       t == KD - 1 and more is None)
                        if h == 1 and more is not None:
                            mm = more()
                        mm.then_inc(dense_done, 1)

                def gate_unit(g, first, j):
                    k = k_gate(first, j)
                    pe.wait_ge(evac_act, act_n(q, g - 1, 8 + j) if j < 2 else act_n(q, g, j - 2))
                    in_unit(g, k, (k if first else k - 4) % 2)

                def x_unit(g, first, j):
                    if j >= 2:
                        pe.wait_ge(evac_act, act_n(q, g, 4 + j - 2))
                    elif first:
                        pe.wait_ge(evac_act, act_n(q, g, 2 + j))
                    else:
                        pe.wait_ge(evac_dve, out_n(q, g, 6 + j))
                    in_unit(g, K_X + j, (K_X + j) % 2)

                def ffn_unit(j):
                    pe.wait_ge(evac_dve, out_n(q, 7, 6 + j) if j < 2 else ffn_n(q, j - 2))
                    more = None
                    if j >= 1:
                        def more():
                            pe.wait_ge(evac_dve, ffn_n(q, 0))
                            return nc.tensor.matmul(bank[(K_X + j) % 2][:], lora_sb[:, (j - 1) * 128:j * 128], w_tok[:],
                                                    start=False, stop=True)
                    in_unit(7, K_X + j, (K_X + j) % 2, more)

                def out_units(g, m, tail=False):
                    k = (K_TAIL if tail else K_OUT) + m
                    for h in range(2):
                        i = 2 * m + h
                        if i >= 2:
                            pe.wait_ge(evac_dve, tail_n(q, i - 2) if tail else out_n(q, g, i - 2))
                        elif tail:
                            pe.wait_ge(evac_dve, ffn_n(q, 7 + i))
                        else:
                            pe.wait_ge(evac_act, act_n(q, g, 2 + i))
                        if i == 0:
                            pe.wait_ge(z_done, chunk(q, g if tail else g - 1, 3) * 2 + (2 + 4))
                        weights(g, k, h)
                        b = ((K_TAIL if tail else 3) + i) % 2
                        for t in range(KZ):
                            mm = three(bank[b][:], w(k, 4 * h + t), (z_hi[:, t, :], z_lo[:, t, :]), t == 0, t == KZ - 1)
                        mm.then_inc(dense_done, 1)

                def chunk_1(g, c, p):
                    n = chunk(q, g, c)
                    cs = slice(c * Q, (c + 1) * Q)
                    if c == 0:
                        pe.wait_ge(post, post_n(q, g, NSET - 1))
                    for j in range(XT):
                        mm = nc.tensor.transpose(pX[:, j * 128:(j + 1) * 128], xT[p][:, j, cs], ident[:])
                    mm.then_inc(s1, 1)
                    nc.tensor.transpose(pCB[:, 0:N], BT[p][:, cs], ident[:])
                    nc.tensor.matmul(pCB[:, N:N + Q], BT[p][:, cs], CT[p][:, cs], start=True, stop=True).then_inc(s1, 1)

                def chunk_2(g, c, p):
                    n = chunk(q, g, c)
                    pe.wait_ge(cs_lo, n + 1)
                    three(pS[:], (C_hi[:], C_lo[:]), (S_hi[:], S_lo[:]), True, True).then_inc(s2, 1)
                    pe.wait_ge(y_step, n * 3 + (0 + CR_2))
                    pe.wait_ge(xw_done, n * 2 + 1)
                    for h in range(HPG):
                        if h % 4 == 0:
                            pe.wait_ge(m_done, n * 2 + (h // 4 + 1))
                        mm = nc.tensor.matmul(pY[:, h * P:(h + 1) * P], E[:, h, :], dtx[:, h * P:(h + 1) * P],
                                              start=True, stop=True)
                    mm.then_inc(s2, 1)

                def chunk_2b(g, c):
                    n = chunk(q, g, c)
                    pe.wait_ge(bl_done, n + 1)
                    pe.wait_ge(wx_lo_done, n + 1)
                    pe.wait_ge(y_step, n * 3 + (1 + CR_2))
                    three(pS[:], (B_hi[:], B_lo[:]), (wx_hi[:], wx_lo[:]), True, True).then_inc(st_done, 1)

                def chunk_3(g, c):
                    n = chunk(q, g, c)
                    pe.wait_ge(z_done, n * 2 + (4 - 1))
                    pe.wait_ge(yn_done, n + 1)
                    for j in range(XT):
                        mm = nc.tensor.transpose(pD0[:, j * 128:(j + 1) * 128], yn[c % 2][:, j * 128:(j + 1) * 128], ident[:])
                    mm.then_inc(s3, 1)

                pe.wait_ge(xn_lo_done, q * (2 * NC) + 2 * NC)
                pe.wait_ge(evac_dve, q * DVE_EV + (-1 + CR_EVAC))
                weights(0, K_DT, 0)
                weights(0, K_DT, 1)
                for t in range(KD):
                    mm = three(bank[0][:], w(K_DT, t), (xn_hi[:, t, :], xn_lo[:, t, :]), t == 0, t == KD - 1)
                mm.then_inc(dense_done, 2)
                for j in range(NSET):
                    if j == 0:
                        pe.wait_ge(evac_dve, q * DVE_EV + (0 + CR_EVAC))
                    elif j == 1:
                        pe.wait_ge(evac_act, q * ACT_EV + (1 + CR_EVAC))
                    else:
                        pe.wait_ge(evac_act, act_n(q, -1, 4 + j - 2))
                    in_unit(0, K_FIRST + j, (1 + j) % 2)
                    if j == 0:
                        pe.wait_ge(evac_act, q * ACT_EV + (1 + CR_EVAC))
                        for i in range(NC):
                            mm = nc.tensor.matmul(pD0[:, i * (H + NE):(i + 1) * (H + NE)], dtT[:, i * 128:(i + 1) * 128],
                                                  ident[:, 0:H + NE], start=True, stop=True)
                        mm.then_inc(lg_done, 1)
                    if j == 3:
                        pe.wait_ge(dt_dve, q * DT_DVE + 17)
                        nc.tensor.matmul(pY[:, 0:NC * H], causal[:], t_a, start=True, stop=True)
                        nc.tensor.matmul(pY[:, NC * H:2 * NC * H], ones[:], t_a, start=True, stop=True)\
                            .then_inc(cum_done, 1)
                    if j == 4:
                        pe.wait_ge(dt_act, q * DT_ACT + 3)
                        for c in range(NC):
                            mm = nc.tensor.matmul(pD1[0:H, c * Q:(c + 1) * Q], tok[:, 4 * NC + c, :], ident[:],
                                                  start=True, stop=True)
                        mm.then_inc(cumT_done, 1)

                def router_transpose():
                    pe.wait_ge(rt_dve, q * RT_DVE + RT_DVE)
                    for i in range(NC):
                        mm = nc.tensor.transpose(pD1[:, i * 128:(i + 1) * 128], w_tok[:, i * 128:(i + 1) * 128], ident[:])
                    mm.then_inc(wT_done, 1)

                def group(g, p, first=False, last=False):
                    def x_units(n):
                        nonlocal j
                        for _ in range(n):
                            ffn_unit(j) if last else x_unit(g, first, j)
                            j += 1

                    def outs(m):
                        if not first:
                            out_units(g, m)

                    j = 0
                    gate_unit(g, first, 0)
                    gate_unit(g, first, 1)
                    chunk_1(g, 0, p)
                    gate_unit(g, first, 2)
                    if not first:
                        chunk_3(g - 1, 3)
                    gate_unit(g, first, 3)
                    n_x = [0, 2, 2, 0, 2, 0, 0] if first else [0, 0, 3, 1, 2, 1, 1] if last else [0, 0, 2, 1, 2, 1, 0]
                    chunk_2(g, 0, p)
                    outs(0)
                    x_units(n_x[0])
                    chunk_2b(g, 0)
                    chunk_1(g, 1, p)
                    outs(1)
                    outs(2)
                    x_units(n_x[1])
                    if last:
                        router_transpose()
                    chunk_2(g, 1, p)
                    chunk_3(g, 0)
                    outs(3)
                    chunk_2b(g, 1)
                    chunk_1(g, 2, p)
                    x_units(n_x[2])
                    chunk_2(g, 2, p)
                    chunk_3(g, 1)
                    x_units(n_x[3])
                    chunk_2b(g, 2)
                    chunk_1(g, 3, p)
                    x_units(n_x[4])
                    chunk_2(g, 3, p)
                    chunk_3(g, 2)
                    x_units(n_x[5])
                    chunk_2b(g, 3)
                    x_units(n_x[6])
                    if last:
                        chunk_3(7, 3)
                        x_units(1)

                group(0, 0, first=True)
                with pe.Fori(0, 3) as pair:
                    group(pair * 2 + 1, 1)
                    group(pair * 2 + 2, 0)
                group(7, 1, last=True)
                ln_transpose(q + 1, 0)
                ln_transpose(q + 1, 1)
                out_units(7, 0, tail=True)
                ln_transpose(q + 1, 2)
                out_units(7, 1, tail=True)
                ln_transpose(q + 1, 3)
                out_units(7, 2, tail=True)
                out_units(7, 3, tail=True)

            with pe.Fori(0, NQ) as q:
                block_body(q)

        @block.vector
        def _(dve):
            for s, n in ((evac_dve, CR_EVAC), (xn_done, CR_2), (y_step, CR_2), (z_done, 4), (s_upd, 1)):
                dve.sem_inc(s, n)
            def lo_second_half(s, n):
                dve.wait_ge(hi_done, n)
                nc.vector.tensor_tensor(w_lo[s][:, 512:1024], w_raw[s][:, 512:1024], w_hi[s][:, 512:1024].bitcast(F32),
                                        ALU.subtract).then_inc(lo1_done, 1)

            def ln_stats(b, i, src=x_next):
                dve.wait_ge(x_loaded[i], (b + 1) * 16)
                for h in range(2):
                    nc.vector.bn_stats(stats[:, i, h, :], src[i][:, 512 * h:512 * h + 512]).then_inc(ln_stat, 1)
                dve.wait_ge(ln_stat, (b * NC + i) * LN_STEPS + 2)
                nc.vector.tensor_tensor(ln_sync[:, i:i + 1], stats[:, i, 0, 1:2], stats[:, i, 1, 1:2], ALU.add)\
                    .then_inc(ln_stat, 1)
                nc.vector.bn_aggr(mv[:, i, :], stats[:, i, :, :].rearrange("p a b -> p (a b)")).then_inc(ln_stat, 1)

            def ln_apply(b, i, src=x_next, dst=xn_next):
                if i >= 2 and dst is xn_next:
                    dve.wait_ge(lnT_done, b * (2 * NC) + (2 * (i - 2) + 2))
                dve.wait_ge(ln_rstd, (b * NC + i) * 2 + 2)
                nc.vector.tensor_scalar(dst[i], src[i], mv[:, i, 0:1], ln_r[:, i, 1:2],
                                        ALU.subtract, ALU.mult).then_inc(xn_done, 1)

            def ln_low(b, i, banks=ln_banks):
                for h in range(2):
                    dve.wait_ge(xn_hi_done, b * (2 * NC) + (2 * i + h + 1))
                    cols = slice(i * 128, (i + 1) * 128)
                    nc.vector.tensor_tensor(xn_lo[:, 4 * h:4 * h + 4, cols],
                                            banks[(2 * i + h) % len(banks)][:].rearrange("p (k t) -> p k t", k=4),
                                            xn_hi[:, 4 * h:4 * h + 4, cols].bitcast(F32), ALU.subtract)\
                        .then_inc(xn_lo_done, 1)

            ln_stats(0, 0, x_first)
            ln_stats(0, 1, x_first)
            ln_apply(0, 0, x_first, xn_first)
            ln_stats(0, 2, x_first)
            ln_apply(0, 1, x_first, xn_first)
            ln_stats(0, 3, x_first)
            ln_apply(0, 2, x_first, xn_first)
            ln_apply(0, 3, x_first, xn_first)
            lo_second_half(0, 2)
            ln_low(0, 0, ln_banks_first)
            ln_low(0, 1, ln_banks_first)
            lo_second_half(1, 4)
            ln_low(0, 2, ln_banks_first)
            ln_low(0, 3, ln_banks_first)
            dve.wait_ge(const_loaded, 96)
            nc.vector.tensor_scalar(consts[:], consts[:], 0.5, None, ALU.mult).then_inc(const_vec, 1)
            dve.wait_ge(const_act, 1)
            nc.vector.tensor_scalar(A_neg[:], A_neg[:], -1.0, None, ALU.mult).then_inc(const_vec, 1)
            dve.wait_ge(const_made, 15)
            dve.wait_ge(const_vec, 2)
            dve.wait_ge(zeroed, 3)

            def heads(t):
                return t.rearrange("t (h p) -> t h p", h=HPG)

            def per_head(kind, c):
                return tok_g[:, kind * NC + c, :].unsqueeze(2).broadcast_to([128, HPG, P])

            def block_body(q):
                n_dt = n_rt = 0

                def dt_step(ins, wait=True):
                    nonlocal n_dt
                    n_dt += 1
                    ins.then_inc(dt_dve, 1)
                    if wait:
                        dve.wait_ge(dt_dve, q * DT_DVE + n_dt)

                def rt_step(ins, wait=True):
                    nonlocal n_rt
                    n_rt += 1
                    ins.then_inc(rt_dve, 1)
                    if wait:
                        dve.wait_ge(rt_dve, q * RT_DVE + n_rt)

                def lo(g, k):
                    lo_second_half(k % 2, q * (2 * SLOTS) + g * (2 * PER_G) + (2 * (k + 2) + 2))

                def conv_taps(g, j):
                    r, n = j % 2, (post_n(q, g + 1, j) - 1) * 4
                    if j >= 2:
                        dve.wait_ge(post, post_n(q, g + 1, j - 2))
                    elif g is not NO_GROUP:
                        dve.wait_ge(gate_done, grp(q, g) * XT + (j + 2 + 1))
                    nc.vector.tensor_copy(conv_in[r][:, 0:3], halo_in[:, j, :]).then_inc(taps, 1)
                    dve.wait_ge(evac_act, act_n(q, g, 4 + j))
                    nc.vector.tensor_copy(halo_out[:, j, :], conv_in[r][:, TB:TB + 3])
                    for t in range(3):
                        dve.wait_ge(taps, n + t + 1)
                        nc.vector.scalar_tensor_tensor(out=conv_u[r], in0=conv_in[r][:, t:t + TB],
                                                       scalar=const_g[:, 4 * j + t:4 * j + t + 1], in1=conv_u[r],
                                                       op0=ALU.mult, op1=ALU.add).then_inc(taps, 1)

                def silu(g, j, p):
                    dve.wait_ge(tanh_done, post_n(q, g + 1, j))
                    dst = xT[p][:, j, :] if j < XT else (BT, CT)[j - XT][p]
                    nc.vector.scalar_tensor_tensor(out=dst, in0=conv_in[j % 2][:, 0:TB], scalar=1.0, in1=conv_u[j % 2],
                                                   op0=ALU.add, op1=ALU.mult).then_inc(post, 1)

                def gate_tile(g, j, first):
                    if j == 0 and not first:
                        dve.wait_ge(z_done, chunk(q, g - 1, 3) * 2 + (1 + 4))
                    dve.wait_ge(evac_act, act_n(q, g, j))
                    nc.vector.scalar_tensor_tensor(out=gate[:, j, :], in0=conv_in[j % 2][:, 0:TB], scalar=1.0,
                                                   in1=conv_u[j % 2], op0=ALU.add, op1=ALU.mult).then_inc(gate_done, 1)

                def chunk_1(g, c):
                    n = chunk(q, g, c)
                    if c == 0:
                        dve.wait_ge(prep_done, q * PREPS + g + 2)
                    dve.wait_ge(ck_evac, n * 2 + 1)
                    nc.vector.tensor_tensor(heads(dtx[:]), heads(x_ck[:]), per_head(0, c), ALU.mult).then_inc(xw_done, 1)
                    nc.vector.tensor_tensor(heads(wx[:]), heads(x_ck[:]), per_head(1, c), ALU.mult).then_inc(xw_done, 1)
                    dve.wait_ge(ck_evac, n * 2 + 2)
                    nc.vector.tensor_tensor(CBm[:], pCB[:, N:N + Q], causal[:], ALU.mult).then_inc(cbm_done, 1)
                    nc.vector.tensor_tensor(B_lo[:], pCB[:, 0:N], B_hi[:].bitcast(F32), ALU.subtract).then_inc(bl_done, 1)
                    dve.wait_ge(cbm_done, n + 1)

                def masked(g, c):
                    n = chunk(q, g, c)
                    for h in range(2):
                        dve.wait_ge(exp_done, n * 2 + (h + 1))
                        nc.vector.tensor_tensor(E[:, 4 * h:4 * h + 4, :], E[:, 4 * h:4 * h + 4, :],
                                                CBm[:].unsqueeze(1).broadcast_to([128, 4, Q]), ALU.mult).then_inc(m_done, 1)

                def chunk_2(g, c):
                    n = chunk(q, g, c)
                    dve.wait_ge(s2, n * 2 + 1)
                    nc.vector.tensor_tensor(heads(y[:]), heads(pS[:]), per_head(2, c), ALU.mult).then_inc(y_step, 1)
                    dve.wait_ge(s2, n * 2 + 2)
                    dve.wait_ge(y_step, n * 3 + (1 + CR_2))
                    nc.vector.tensor_tensor(y[:], y[:], pY[:], ALU.add).then_inc(y_step, 1)
                    dve.wait_ge(xd_done, n + 1 + 1)
                    dve.wait_ge(y_step, n * 3 + (2 + CR_2))
                    nc.vector.tensor_tensor(y[:], y[:], xD[:], ALU.add).then_inc(y_step, 1)

                def normalize(g, c):
                    n = chunk(q, g, c)
                    dve.wait_ge(rstd_done, n * 2 + 2)
                    nc.vector.tensor_scalar(yn[c % 2][:], y[:], rstd[:, 1:2], None, ALU.mult).then_inc(yn_done, 1)

                def state(g, c):
                    n = chunk(q, g, c)
                    dve.wait_ge(sdec_done, n + 1)
                    dve.wait_ge(st_done, n + 1)
                    nc.vector.tensor_tensor(S_cur[:], S_dec[:], pS[:], ALU.add).then_inc(s_upd, 1)

                def gated(g, c):
                    n = chunk(q, g, c)
                    if c == 0:
                        dve.wait_ge(gate_done, grp(q, g) * XT + XT)
                    dve.wait_ge(s3, n + 1)
                    nc.vector.tensor_tensor(z_t[:], pD0[:].rearrange("p (j t) -> p j t", j=XT),
                                            gate[:, :, c * Q:(c + 1) * Q], ALU.mult).then_inc(z_done, 1)

                def gated_lo(g, c):
                    n = chunk(q, g, c)
                    dve.wait_ge(zhi_done, n + 1)
                    cs = slice(c * Q, (c + 1) * Q)
                    nc.vector.tensor_tensor(z_lo[:, :, cs], z_t[:], z_hi[:, :, cs].bitcast(F32), ALU.subtract)\
                        .then_inc(z_done, 1)

                def out_adds(g, m, tail=False):
                    for h in range(2):
                        i = 2 * m + h
                        dve.wait_ge(dense_done, dense_n(q, g, (K_TAIL if tail else K_OUT) + m, h))
                        n = tail_n(q, i) if tail else out_n(q, g, i)
                        dve.wait_ge(evac_dve, n - 2)
                        b = ((K_TAIL if tail else 3) + i) % 2
                        nc.vector.tensor_tensor(acc[:, i, :], acc[:, i, :], bank[b][:], ALU.add).then_inc(evac_dve, 1)

                def ffn_evac(j):
                    b = (K_X + j) % 2
                    dve.wait_ge(dense_done, dense_n(q, 7, K_X + j, 1))
                    dve.wait_ge(evac_dve, ffn_n(q, j - 2))
                    if j == 0:
                        dve.wait_ge(w_tok_ready, q + 1)
                        nc.vector.tensor_tensor(w_tok[:], w_tok[:], bank[b][:], ALU.mult).then_inc(evac_dve, 1)
                    else:
                        nc.vector.scalar_tensor_tensor(out=acc[:, j - 1, :], in0=bank[b][:], scalar=bb[:, j - 1:j],
                                                       in1=acc[:, j - 1, :], op0=ALU.add, op1=ALU.add).then_inc(evac_dve, 1)

                def prep(g):
                    nc.vector.tensor_scalar(tok_g[:], tok[:, :, bass.ds(g * HPG, HPG)], 1.0, None, ALU.mult)
                    nc.vector.tensor_scalar(D_g[:], D_all[:, bass.ds(g * HPG, HPG)], 1.0, None, ALU.mult)
                    nc.vector.tensor_scalar(const_g[:], consts[:, bass.ds(g + 1, 1), :].rearrange("p a c -> p (a c)"),
                                            1.0, None, ALU.mult)
                    nc.vector.tensor_scalar(halo[:, bass.ds(g, 1), :, :].rearrange("p a j t -> p (a j t)"),
                                            halo_out[:].rearrange("p j t -> p (j t)"), 1.0, None, ALU.mult)
                    nc.vector.tensor_scalar(halo_in[:].rearrange("p j t -> p (j t)"),
                                            halo[:, bass.ds(g + 1, 1), :, :].rearrange("p a j t -> p (a j t)"),
                                            1.0, None, ALU.mult).then_inc(prep_done, 1)
                    dve.wait_ge(s_upd, grp(q, g) * S_STEPS + 1)
                    nc.vector.tensor_scalar(S_cur[:], S_all[:, bass.ds(g, 1), :].rearrange("p a c -> p (a c)"),
                                            1.0, None, ALU.mult).then_inc(s_upd, 1)

                def save_state(g):
                    dve.wait_ge(s_upd, grp(q, g) * S_STEPS + (5 + 1))
                    nc.vector.tensor_scalar(S_all[:, bass.ds(g, 1), :].rearrange("p a c -> p (a c)"), S_cur[:],
                                            1.0, None, ALU.mult).then_inc(s_upd, 1)

                nc.vector.tensor_copy(const_g[:], consts[:, 0, :])
                nc.vector.tensor_copy(halo_in[:], halo[:, 0, :, :]).then_inc(prep_done, 1)
                def by_head(t):
                    return t.rearrange("p (c h) -> p c h", c=NC)

                rows = pD0[:, 0:NC * (H + NE)].rearrange("p (i e) -> p i e", i=NC)
                dve.wait_ge(lg_done, q + 1)
                dt_step(nc.vector.tensor_tensor(by_head(t_v), rows[:, :, 0:H], dtb[:].unsqueeze(1).broadcast_to([128, NC, H]),
                                                ALU.add), wait=False)
                dve.wait_ge(prep_done, q * PREPS + 1)
                conv_taps(NO_GROUP, 0)
                dve.wait_ge(dt_act, q * DT_ACT + 2)
                dt_step(nc.vector.tensor_scalar(t_p, t_e, 2.0, None, ALU.add))
                dt_step(nc.vector.reciprocal(t_r, t_p))
                dt_step(nc.vector.tensor_tensor(t_z, t_e, t_r, ALU.mult))
                dt_step(nc.vector.tensor_tensor(t_z2, t_z, t_z, ALU.mult))
                dt_step(nc.vector.tensor_scalar(t_p, t_z2, 1.0 / 15, None, ALU.mult))
                for d in (13, 11):
                    dt_step(nc.vector.scalar_tensor_tensor(out=t_p, in0=t_p, scalar=1.0 / d, in1=t_z2, op0=ALU.add,
                                                           op1=ALU.mult))
                silu(-1, 0, 0)
                conv_taps(NO_GROUP, 1)
                for d in (9, 7, 5, 3):
                    dt_step(nc.vector.scalar_tensor_tensor(out=t_p, in0=t_p, scalar=1.0 / d, in1=t_z2, op0=ALU.add,
                                                           op1=ALU.mult))
                dt_step(nc.vector.scalar_tensor_tensor(out=t_p, in0=t_p, scalar=1.0, in1=t_z, op0=ALU.add, op1=ALU.mult))
                dt_step(nc.vector.tensor_scalar(t_v, t_v, 0.0, None, ALU.max))
                dt_step(nc.vector.scalar_tensor_tensor(out=tk_dt, in0=t_p, scalar=2.0, in1=t_v, op0=ALU.mult, op1=ALU.add))
                dt_step(nc.vector.tensor_tensor(by_head(t_a), by_head(tk_dt), A_neg[:].unsqueeze(1).broadcast_to([128, NC, H]),
                                                ALU.mult))
                dt_step(nc.vector.tensor_scalar(t_a, t_a, LOG_ZERO, None, ALU.max), wait=False)
                silu(-1, 1, 0)
                conv_taps(NO_GROUP, 2)
                silu(-1, 2, 0)
                conv_taps(NO_GROUP, 3)
                dve.wait_ge(dt_act, q * DT_ACT + 5)
                dt_step(nc.vector.tensor_tensor(t_diff, pY[:, NC * H:2 * NC * H], tk_cum, ALU.subtract), wait=False)
                silu(-1, 3, 0)
                conv_taps(NO_GROUP, 4)
                dve.wait_ge(dt_act, q * DT_ACT + 6)
                dt_step(nc.vector.tensor_tensor(tk_w, tk_dt, t_e, ALU.mult), wait=False)
                silu(-1, 4, 0)
                conv_taps(NO_GROUP, 5)
                silu(-1, 5, 0)
                dve.wait_ge(dt_dve, q * DT_DVE + DT_DVE)
                dve.wait_ge(lo1_done, q * SLOTS + (NSET + 3))
                prep(0)
                assert n_dt == DT_DVE, n_dt

                def router_top():
                    lg = rows[:, :, H:H + NE]
                    for i in range(NC):
                        rt_step(nc.vector.max(m8[:, i, :], lg[:, i, :]), wait=i == NC - 1)
                    rt_step(nc.vector.tensor_tensor(pr[:, 0, :], m8[:, :, 1], m8[:, :, 0], ALU.subtract), wait=False)
                    for i in range(NC):
                        rt_step(nc.vector.max_index(ix8[:, i, :], m8[:, i, :], lg[:, i, :]), wait=i == NC - 1)
                    rt_step(nc.vector.tensor_copy(ixf[:], ix8[:, :, 0:2]), wait=False)

                def router_weights():
                    dve.wait_ge(rt_act, q + 1)
                    dve.wait_ge(rt_dve, q * RT_DVE + 10)
                    rt_step(nc.vector.tensor_scalar(pr[:, 2, :], pr[:, 1, :], 1.0, 0.5, ALU.add, ALU.mult))
                    rt_step(nc.vector.reciprocal(pr[:, 2, :], pr[:, 2, :]))
                    rt_step(nc.vector.tensor_tensor(pr[:, 3, :], pr[:, 1, :], pr[:, 2, :], ALU.mult))
                    for s in range(2):
                        rt_step(nc.vector.tensor_tensor(rw[:, s], iota[:].unsqueeze(1).broadcast_to([128, NC, NE]),
                                                        ixf[:, :, s:s + 1].broadcast_to([128, NC, NE]), ALU.is_equal),
                                wait=s == 1)
                    for s in range(2):
                        rt_step(nc.vector.tensor_tensor(rw[:, s], rw[:, s], pr[:, 2 + s, :].unsqueeze(2)
                                                        .broadcast_to([128, NC, NE]), ALU.mult), wait=s == 1)
                    rt_step(nc.vector.tensor_tensor(rw[:, 2], rw[:, 0], rw[:, 1], ALU.add))
                    rt_step(nc.vector.tensor_copy(w_tok[:].rearrange("t (e r) -> t e r", r=RANK),
                                                  rw[:, 2].rearrange("p i e -> p (i e)").unsqueeze(2)
                                                  .broadcast_to([128, NC * NE, RANK])), wait=False)
                    assert n_rt == RT_DVE, n_rt

                def group(g, p, first=False, last=False):
                    def out_unit(m):
                        if not first:
                            if m == 0:
                                dve.wait_ge(acc_loaded, (q + 1) * 16)
                            out_adds(g, m)
                            lo(g, K_OUT + m)

                    def x_low(j):
                        if last:
                            ffn_evac(j)
                        lo(g, K_X + j)

                    def x_conv(j):
                        if not last:
                            conv_taps(g, j)
                            if j >= 1:
                                silu(g, j - 1, 1 - p)

                    def x_unit(j):
                        x_low(j)
                        x_conv(j)

                    lo(g, k_gate(first, 0))
                    lo(g, k_gate(first, 1))
                    chunk_1(g, 0)
                    masked(g, 0)
                    lo(g, k_gate(first, 2))
                    if not first:
                        gated(g - 1, 3)
                    gate_tile(g, 0, first)
                    gate_tile(g, 1, first)
                    if not first:
                        gated_lo(g - 1, 3)
                    gate_tile(g, 2, first)
                    lo(g, k_gate(first, 3))
                    chunk_2(g, 0)
                    gate_tile(g, 3, first)
                    out_unit(0)
                    state(g, 0)
                    if first:
                        router_top()
                    normalize(g, 0)
                    chunk_1(g, 1)
                    out_unit(1)
                    masked(g, 1)
                    out_unit(2)
                    if first:
                        x_unit(0)
                    chunk_2(g, 1)
                    gated(g, 0)
                    out_unit(3)
                    state(g, 1)
                    if first:
                        x_unit(1)
                    normalize(g, 1)
                    gated_lo(g, 0)
                    chunk_1(g, 2)
                    masked(g, 2)
                    x = [2, 3] if first else [1, 2] if last else [0, 1]
                    if last:
                        x_unit(0)
                    x_unit(x[0])
                    if not first:
                        x_low(x[1])
                    chunk_2(g, 2)
                    gated(g, 1)
                    if first:
                        state(g, 2)
                        x_low(x[1])
                    x_conv(x[1])
                    gated_lo(g, 1)
                    if not first:
                        x_low(x[1] + 1)
                        state(g, 2)
                        x_conv(x[1] + 1)
                    normalize(g, 2)
                    chunk_1(g, 3)
                    masked(g, 3)
                    if last:
                        ln_stats(q + 1, 0)
                        ln_stats(q + 1, 1)
                    x = [4, 5] if first or last else [3, 4]
                    x_unit(x[0])
                    if not first:
                        x_low(x[1])
                    if last:
                        ln_apply(q + 1, 0)
                        ln_apply(q + 1, 1)
                    chunk_2(g, 3)
                    gated(g, 2)
                    if first:
                        state(g, 3)
                        x_low(x[1])
                    x_conv(x[1])
                    gated_lo(g, 2)
                    if not first:
                        x_low(x[1] + 1)
                        state(g, 3)
                        x_conv(x[1] + 1)
                    normalize(g, 3)
                    save_state(g)
                    if last:
                        x_unit(7)
                        ln_stats(q + 1, 2)
                        gated(7, 3)
                        gated_lo(7, 3)
                        ln_stats(q + 1, 3)
                        x_unit(8)
                    else:
                        silu(g, 5, 1 - p)
                        prep(g + 1)
                    if first:
                        router_weights()

                group(0, 0, first=True)
                with dve.Fori(0, 3) as pair:
                    group(pair * 2 + 1, 1)
                    group(pair * 2 + 2, 0)
                group(7, 1, last=True)
                ln_low(q + 1, 0)
                ln_apply(q + 1, 2)
                ln_low(q + 1, 1)
                ln_apply(q + 1, 3)
                for m in range(4):
                    out_adds(7, m, tail=True)
                    lo(7, K_TAIL + m)
                    if m < 2:
                        ln_low(q + 1, m + 2)

            with dve.Fori(0, NQ) as q:
                block_body(q)


def _tile_slot(np, rows):
    return np.ascontiguousarray(rows.reshape(128, KD, 128).transpose(2, 1, 0)).reshape(128, KD * 128)


def _pack_weights(np, w_in, w_router, w_out, w_base, lora_a):
    gate_r, x_r, b_r, c_r, dt_r = 0, I, 2 * I, 2 * I + G * N, 2 * I + 2 * G * N
    dt_rows = np.zeros((128, DM), w_in.dtype)
    dt_rows[:H] = w_in[dt_r:dt_r + H]
    dt_rows[H:H + NE] = w_router
    slots = [_tile_slot(np, dt_rows)]

    def conv_set(g):
        for j in range(XT):
            r = x_r + g * GC + j * 128
            slots.append(_tile_slot(np, w_in[r:r + 128]))
        for base in (b_r, c_r):
            slots.append(_tile_slot(np, w_in[base + g * N:base + (g + 1) * N]))

    def out_set(g):
        for m in range(OT // 2):
            part = w_out[m * 256:(m + 1) * 256, g * GC:(g + 1) * GC].reshape(2, 128, KZ, 128)
            slots.append(np.ascontiguousarray(part.transpose(3, 0, 2, 1)).reshape(128, 1024))

    conv_set(0)
    for g in range(G):
        for j in range(XT):
            r = gate_r + g * GC + j * 128
            slots.append(_tile_slot(np, w_in[r:r + 128]))
        if g >= 1:
            out_set(g - 1)
        if g < G - 1:
            conv_set(g + 1)
        else:
            slots.append(_tile_slot(np, lora_a.reshape(NE * RANK, DM)))
            for o in range(OT):
                slots.append(_tile_slot(np, w_base[o * 128:(o + 1) * 128]))
    out_set(G - 1)
    assert len(slots) == SLOTS
    return np.stack(slots + slots[:2])


def _pack_group_consts(np, conv_w, conv_b, norm_w):
    out = np.zeros((128, G + 1, NCONST), conv_w.dtype)
    for g in range(G):
        starts = [g * GC + j * 128 for j in range(XT)] + [I + g * N, I + G * N + g * N]
        for j, r in enumerate(starts):
            out[:, g, 4 * j:4 * j + 4] = conv_w[r:r + 128]
            out[:, g, BIAS0 + j] = conv_b[r:r + 128]
        for j in range(XT):
            out[:, g + 1, NORM0 + j] = norm_w[g * GC + j * 128:g * GC + (j + 1) * 128]
    return out


def kernel(**inputs):
    import numpy as np
    import concourse.bacc as bacc
    from concourse.bass_utils import run_bass_kernel_spmd as run

    a = {k: np.ascontiguousarray(v) for k, v in inputs.items()}
    x = a["L0_attn_hidden_states"].reshape(L, DM)
    arrays = {
        "x_tok_dram": np.concatenate([x, x[:TB]]),
        "x_tr_dram": np.ascontiguousarray(x.reshape(NQ, TB, OT, 128).transpose(0, 3, 2, 1)),
        "w_slots_dram": _pack_weights(np, a["L0_attn_in_proj_w"], a["L0_ffn_W_router"], a["L0_attn_out_proj_w"],
                                      a["L0_ffn_W_base"], a["L0_ffn_A"]),
        "group_const_dram": _pack_group_consts(np, a["L0_attn_conv_weight"], a["L0_attn_conv_bias"],
                                               a["L0_attn_norm_weight"]),
        "dt_bias_dram": np.ascontiguousarray(np.broadcast_to(a["L0_attn_dt_bias"], (128, H))),
        "a_log_dram": np.ascontiguousarray(np.broadcast_to(a["L0_attn_A_log"], (128, H))),
        "d_skip_dram": np.ascontiguousarray(np.broadcast_to(a["L0_attn_D"], (128, H))),
        "b_base_dram": np.ascontiguousarray(a["L0_ffn_b_base"].reshape(OT, 128).T),
        "lora_b_dram": np.ascontiguousarray(a["L0_ffn_B"].transpose(0, 2, 1)).reshape(NE * RANK, DM),
    }
    nc = bacc.Bacc("TRN2", target_bir_lowering=False, num_devices=1)
    args = [nc.dram_tensor(n, v.shape, mybir.dt.from_np(v.dtype), kind="ExternalInput").ap() for n, v in arrays.items()]
    args.append(nc.dram_tensor("out_tr_dram", (NQ, 128, OT, TB), F32, kind="ExternalOutput").ap())
    layer_kernel(nc, *args)
    r = run(nc, [arrays], core_ids=[0])
    out = r.results[0]["out_tr_dram"]
    return np.ascontiguousarray(out.transpose(0, 3, 2, 1)).reshape(1, L, DM)
```
